# Optimizing a Trainium2 kernel written in Bass

```python
import numpy as np
import jax
import jax.numpy as jnp

def _softmax(x, axis=-1):
    return jax.nn.softmax(x, axis=axis)

def _gelu(x):
    return jax.nn.gelu(x, approximate=True)

def _silu(x):
    return jax.nn.silu(x)

def _sigmoid(x):
    return jax.nn.sigmoid(x)

def _layernorm(x, axis=-1, eps=1e-05):
    m = jnp.mean(x, axis=axis, keepdims=True)
    v = jnp.var(x, axis=axis, keepdims=True)
    return (x - m) / jnp.sqrt(v + eps)

def _scatter_add(tgt, idx, src, axis=0):
    return tgt.at[idx].add(src)

def _segment_sum(src, seg, n):
    return jax.ops.segment_sum(src, seg, n)
kernel_name = 'mk_adj_preln_d4_adj_r2_9d6167'

def setup_inputs(seed: int=0):
    np.random.seed(seed)
    _w = jnp.asarray

    def _rec_inputs():
        import jax
        import jax.numpy as jnp
        _gk = jax.random.key(seed)
        x = -0.000929 + 1 * jax.random.normal(jax.random.fold_in(_gk, 1), (4096, 128), jnp.float32)
        _a = jax.random.bernoulli(jax.random.fold_in(_gk, 2), 0.000488281, (4096, 4096))
        _a = jnp.logical_or(_a, jnp.swapaxes(_a, -1, -2))
        _a = jnp.logical_or(_a, jnp.eye(4096, dtype=bool))
        _af = _a.astype(jnp.float32)
        _af = _af * jax.random.uniform(jax.random.fold_in(_gk, 3), (4096, 4096), jnp.float32, 0.05, 1)
        adj = _af
        return (x, adj)
    x, adj = _rec_inputs()

    def _L0_gnn_setup():
        import jax, jax.numpy as jnp
        import numpy as np
        N = 4096
        H = 128
        key = jax.random.key(seed)
        k_x, k_A, k_W = jax.random.split(key, 3)
        x = jax.random.normal(k_x, (N, H), dtype=jnp.float32)
        A = jax.random.uniform(k_A, (N, N), dtype=jnp.float32)
        alpha = jnp.array([0.5], dtype=jnp.float32)
        bound = 1.0 / np.sqrt(H)
        W = jax.random.uniform(k_W, (H, H), dtype=jnp.float32, minval=-bound, maxval=bound)
        b = jnp.zeros((H,), dtype=jnp.float32)
        t = jnp.zeros((1,), dtype=jnp.float32)
        return {'t': t, 'x': x, 'A': A, 'alpha': alpha, 'W': W, 'b': b}
    _L0_gnn_all = _L0_gnn_setup()
    _L0_gnn_in = {k: v for k, v in _L0_gnn_all.items() if k in ('t', 'alpha', 'W', 'b')}
    del _L0_gnn_all

    def _L1_gnn_setup():
        import jax, jax.numpy as jnp
        import numpy as np
        K = 2
        NEG = -9000000000000000.0
        N, C, CO = (3072, 128, 128)

        def _ln(x, g, b, eps=1e-05):
            m = x.mean(-1, keepdims=True)
            v = ((x - m) ** 2).mean(-1, keepdims=True)
            return (x - m) / jnp.sqrt(v + eps) * g + b
        key = jax.random.key(seed)
        ks = jax.random.split(key, 6)
        x = jax.random.normal(ks[0], (N, C), jnp.float32)
        adj = (jax.random.uniform(ks[1], (N, N)) < 0.01).astype(jnp.float32)
        ff0_w = jax.random.normal(ks[2], (K, C, C), jnp.float32) / np.float32(np.sqrt(C))
        ff1_w = jax.random.normal(ks[3], (K, CO, C), jnp.float32) / np.float32(np.sqrt(C))
        attn_w = jax.random.normal(ks[4], (K, 2 * C), jnp.float32) / np.float32(np.sqrt(2 * C))
        return dict(x=x, adj=adj, ff0_w=ff0_w, ff1_w=ff1_w, attn_w=attn_w, g1=jnp.ones((C,), jnp.float32), b1=jnp.zeros((C,), jnp.float32), g2=jnp.ones((C,), jnp.float32), b2=jnp.zeros((C,), jnp.float32))
    _L1_gnn_all = _L1_gnn_setup()
    _L1_gnn_in = {k: v for k, v in _L1_gnn_all.items() if k in ('ff0_w', 'ff1_w', 'attn_w', 'g1', 'b1', 'g2', 'b2')}
    del _L1_gnn_all

    def _L2_gnn_setup():
        import jax, jax.numpy as jnp
        import numpy as np
        N, D = (4096, 128)
        EDGE_P = 0.004
        NEG = -9000000000000000.0
        LRELU_ALPHA = 0.2
        key = jax.random.key(seed)
        k1, k2, k3, k4, k5 = jax.random.split(key, 5)
        inputs = jax.random.normal(k1, (N, D), jnp.float32)
        adj = (jax.random.uniform(k2, (N, N)) < EDGE_P).astype(jnp.float32)
        idx = jnp.arange(N)
        adj = adj.at[idx, idx].set(1.0)
        cmt_weight = jax.random.normal(k3, (N,), jnp.float32)
        W = jax.random.normal(k4, (D, D), jnp.float32) / np.sqrt(D)
        a = jax.random.normal(k5, (2 * D,), jnp.float32) / np.sqrt(2.0 * D)
        return {'inputs': inputs, 'adj': adj, 'cmt_weight': cmt_weight, 'W': W, 'a': a}
    _L2_gnn_all = _L2_gnn_setup()
    _L2_gnn_in = {k: v for k, v in _L2_gnn_all.items() if k in ('cmt_weight', 'W', 'a')}
    del _L2_gnn_all

    def _L3_gnn_setup():
        import jax, jax.numpy as jnp
        import numpy as np
        N, E, D = (4096, 4096, 128)
        key = jax.random.key(seed)
        k1, k2 = jax.random.split(key)
        X = jax.random.normal(k1, (N, D), dtype=jnp.float32)
        H = jax.random.uniform(k2, (N, E), dtype=jnp.float32)
        return {'X': X, 'H': H}
    _L3_gnn_all = _L3_gnn_setup()
    _L3_gnn_in = {k: v for k, v in _L3_gnn_all.items() if k in ()}
    del _L3_gnn_all
    return {'x': x, 'adj': adj, 'L0_gnn_t': _L0_gnn_in['t'], 'L0_gnn_alpha': _L0_gnn_in['alpha'], 'L0_gnn_W': _L0_gnn_in['W'], 'L0_gnn_b': _L0_gnn_in['b'], 'L1_gnn_ff0_w': _L1_gnn_in['ff0_w'], 'L1_gnn_ff1_w': _L1_gnn_in['ff1_w'], 'L1_gnn_attn_w': _L1_gnn_in['attn_w'], 'L1_gnn_g1': _L1_gnn_in['g1'], 'L1_gnn_b1': _L1_gnn_in['b1'], 'L1_gnn_g2': _L1_gnn_in['g2'], 'L1_gnn_b2': _L1_gnn_in['b2'], 'L2_gnn_cmt_weight': _L2_gnn_in['cmt_weight'], 'L2_gnn_W': _L2_gnn_in['W'], 'L2_gnn_a': _L2_gnn_in['a']}

def reference(x, adj, L0_gnn_t, L0_gnn_alpha, L0_gnn_W, L0_gnn_b, L1_gnn_ff0_w, L1_gnn_ff1_w, L1_gnn_attn_w, L1_gnn_g1, L1_gnn_b1, L1_gnn_g2, L1_gnn_b2, L2_gnn_cmt_weight, L2_gnn_W, L2_gnn_a):
    import jax
    import jax.numpy as jnp

    def _L0_gnn_ref(t, x, A, alpha, W, b):
        import jax, jax.numpy as jnp
        import numpy as np
        N = 4096
        H = 128
        a = alpha[0]
        A_prime = a * A
        diag = jnp.diagonal(A_prime) + (1.0 - a)
        A_prime = A_prime.at[jnp.arange(N), jnp.arange(N)].set(diag)
        out_degree = A_prime.sum(axis=1)
        inv_deg = jnp.where(out_degree == 0.0, 0.0, 1.0 / out_degree)
        x = inv_deg[:, None] * A_prime @ x
        x = x @ W.T + b
        return jax.nn.relu(x)

    def _L1_gnn_ref(x, adj, ff0_w, ff1_w, attn_w, g1, b1, g2, b2):
        import jax, jax.numpy as jnp
        import numpy as np
        K = 2
        NEG = -9000000000000000.0
        N, C, CO = (3072, 128, 128)

        def _ln(x, g, b, eps=1e-05):
            m = x.mean(-1, keepdims=True)
            v = ((x - m) ** 2).mean(-1, keepdims=True)
            return (x - m) / jnp.sqrt(v + eps) * g + b
        n, c = x.shape
        co = ff1_w.shape[1]
        x_norm = _ln(x, g1, b1)
        mask = (adj > 0) | jnp.eye(n, dtype=bool)
        h_next = jnp.zeros((n, co), x.dtype)
        for i in range(K):
            h = x_norm @ ff0_w[i].T
            s_src = h @ attn_w[i, :c]
            s_dst = h @ attn_w[i, c:]
            e = jax.nn.leaky_relu(s_src[:, None] + s_dst[None, :])
            e = jnp.where(mask, e, jnp.float32(NEG))
            atten = jax.nn.softmax(e, axis=1)
            att = atten @ h + x
            att = _ln(att, g2, b2)
            h_next = h_next + jax.nn.elu(att @ ff1_w[i].T) / K
        return h_next

    def _L2_gnn_ref(inputs, adj, cmt_weight, W, a):
        import jax, jax.numpy as jnp
        import numpy as np
        N, D = (4096, 128)
        EDGE_P = 0.004
        NEG = -9000000000000000.0
        LRELU_ALPHA = 0.2
        Wh = inputs @ W
        f_src = Wh @ a[:D]
        f_dst = Wh @ a[D:]
        e = jax.nn.leaky_relu(f_src[:, None] + f_dst[None, :], LRELU_ALPHA)
        e = jnp.where(adj > 0, e, NEG)
        att = jax.nn.softmax(e, axis=-1)
        return jax.nn.relu(att @ Wh)

    def _L3_gnn_ref(X, H):
        import jax, jax.numpy as jnp
        import numpy as np
        N, E, D = (4096, 4096, 128)
        msg = jnp.matmul(H.T, X)
        inv_deg = 1.0 / H.sum(axis=0)
        inv_deg = jnp.where(jnp.isinf(inv_deg), 0.0, inv_deg)
        return msg * inv_deg[:, None]
    h = jnp.maximum(_layernorm(x, axis=-1), 0.0)
    x = x + _L0_gnn_ref(L0_gnn_t, h, adj, L0_gnn_alpha, L0_gnn_W, L0_gnn_b)
    h = jnp.maximum(_layernorm(x, axis=-1), 0.0)
    x = x + _L1_gnn_ref(h, adj, L1_gnn_ff0_w, L1_gnn_ff1_w, L1_gnn_attn_w, L1_gnn_g1, L1_gnn_b1, L1_gnn_g2, L1_gnn_b2)
    h = jnp.maximum(_layernorm(x, axis=-1), 0.0)
    x = x + _L2_gnn_ref(h, adj, L2_gnn_cmt_weight, L2_gnn_W, L2_gnn_a)
    h = jnp.maximum(_layernorm(x, axis=-1), 0.0)
    x = x + _L3_gnn_ref(h, adj)
    return x

_drawn_inputs = setup_inputs


def setup_inputs(seed=0):
    import zlib

    import numpy as np

    out = dict(_drawn_inputs(seed))
    spreads = {'L0_gnn_b': (0.0, 0.1),
     'L1_gnn_g1': (1.0, 0.2),
     'L1_gnn_b1': (0.0, 0.1),
     'L1_gnn_g2': (1.0, 0.2),
     'L1_gnn_b2': (0.0, 0.1)}
    factors = {}
    for name, (base, spread) in spreads.items():
        noise = np.random.default_rng([zlib.crc32(name.encode()), seed]).standard_normal(out[name].shape)
        drawn = base * np.exp(spread * noise) if base else spread * noise
        out[name] = jnp.asarray(drawn.astype(out[name].dtype))
    for name, factor in factors.items():
        out[name] = (out[name] * factor).astype(out[name].dtype)
    return out
```

```python
from contextlib import ExitStack

import concourse.bass as bass
from concourse import mybir

P = 128
ALU = mybir.AluOpType
ACT = mybir.ActivationFunctionType
F32 = mybir.dt.float32
U8 = mybir.dt.uint8
AX_X = mybir.AxisListType.X
EPS = 1e-5
SLOPES = [0.01, 0.01, 0.2]


class Steps:

    def __init__(self, eng, sem):
        self.eng, self.sem, self.done, self.extra = eng, sem, 0, None

    def mark(self, ins):
        ins.then_inc(self.sem, 1)
        self.done += 1

    def wait(self):
        self.eng.wait_ge(self.sem, self.done if self.extra is None else self.extra + self.done)

    def then(self, ins):
        self.mark(ins)
        self.wait()

    def enter(self, turn, per_turn):
        self.start, self.per_turn, self.extra = self.done, per_turn, turn * per_turn

    def leave(self, turns):
        assert self.done - self.start == self.per_turn, (self.done - self.start, self.per_turn)
        self.done, self.extra = self.start + self.per_turn * turns, None


def graph_layers(nc, x, adj, adj_t, diag, alpha, w0_t, bias0, ff0, ff0_t, ff1_t, attn, g1, b1, g2, b2,
                 w2, w2_t, a2, out):
    N, D = x.shape
    T = N // P
    Q = 4
    S = T // Q
    QC = S * P
    DW = D + 1
    PW = D + 2
    HEADS = 2
    BANK = 512
    NB = (S + 2) // 3
    STREAM = 4
    DEEP = 8
    RUNS1 = Q
    RUNS2 = RUNS1 + HEADS * Q
    RUNS3 = RUNS2 + Q

    with ExitStack() as ctx:
        def sb(name, shape, dt=F32):
            return ctx.enter_context(nc.sbuf_tensor(name, shape, dt))

        def sem(name):
            return ctx.enter_context(nc.semaphore(name))

        mask = sb("mask", [P, T * N], U8)
        X = sb("X", [P, T, D])
        G = sb("G", [P, HEADS, T, DW])
        ring = sb("ring", [P, 5, QC])
        U = sb("U", [P, S * DW])
        V = sb("V", [P, S, D])
        ident = sb("ident", [P, P])
        ff1T = sb("ff1T", [P, HEADS, D])
        rank = sb("rank", [P, 3, T])
        row = sb("row", [P, 3, T])
        norm_scale = sb("norm_scale", [P, T])
        norm_shift = sb("norm_shift", [P, T])
        stats = sb("stats", [P, S, 6])
        mean = sb("mean", [P, S])
        parts = sb("parts", [P, 3, S])
        var = sb("var", [P, S])
        dev = sb("dev", [P, S])
        scale = sb("scale", [P, S])
        shift = sb("shift", [P, S])
        cols = sb("cols", [P, 32])
        rq = sb("rq", [P, S])
        inv = sb("inv", [P, S])
        zero = sb("zero", [P, S])
        dsub = sb("dsub", [P, T])

        E = [ring[:, i, :] for i in range(2)]
        R = [ring[:, 2 + i, :] for i in range(2)]
        elu0 = ring[:, 4, :].rearrange("p (s d) -> p s d", d=D)
        spare = ring[:, 4, :]
        w0T = spare[:, 0:D]
        bias0_b = spare[:, D:2 * D]
        proj1 = [spare[:, 2 * D + h * PW:2 * D + (h + 1) * PW] for h in range(HEADS)]
        o = 2 * D + HEADS * PW
        ff0raw = [spare[:, o + h * D:o + (h + 1) * D] for h in range(HEADS)]
        w2raw = spare[:, o + 2 * D:o + 3 * D]
        proj2 = spare[:, 0:PW]
        mean2 = spare[:, PW:PW + D]
        stream3 = mask[:, 0:DEEP * QC * 4].bitcast(F32).rearrange("p (s c) -> p s c", c=QC)
        U3 = U[:, :].rearrange("p (s d) -> p s d", d=DW)
        g1c, b1c, g2c, b2c, alphac, restc, top, bigc, wbias, vbias = [cols[:, i:i + 1] for i in range(10)]
        twice, apart, squares = [parts[:, i, :] for i in range(3)]
        attnc = cols[:, 10:16]
        qv = cols[:, 16:22]
        hsum = cols[:, 22:26]
        hmean = cols[:, 26:27]

        acc = ctx.enter_context(nc.psum_tensor("acc", [P, NB, BANK], F32))
        turn = ctx.enter_context(nc.psum_tensor("turn", [P, 2 * BANK], F32))
        mix = ctx.enter_context(nc.psum_tensor("mix", [P, NB, BANK], F32))
        mixed = mix[:, 0:2, :].rearrange("p b c -> p (b c)")
        mixed3 = mixed.rearrange("p (s d) -> p s d", d=D)
        one = mix[:, 2, 0:P]

        x_loaded, weights_loaded, w2_loaded, stored = sem("x_loaded"), sem("weights_loaded"), sem("w2_loaded"), sem("stored")
        slot_loaded = [sem(f"slot_loaded{i}") for i in range(STREAM)]
        deep_loaded = [sem(f"deep_loaded{i}") for i in range(DEEP)]
        consts_made, ident_zero = sem("consts_made"), sem("ident_zero")
        dve_step, act_step = sem("dve_step"), sem("act_step")
        qv_summed, qv_placed, qv2_placed = sem("qv_summed"), sem("qv_placed"), sem("qv2_placed")
        p_var, p_dev, p_scale, p_norm = sem("p_var"), sem("p_dev"), sem("p_scale"), sem("p_norm")
        p2_var, p2_dev, p2_scale, p2_in = sem("p2_var"), sem("p2_dev"), sem("p2_scale"), sem("p2_in")
        p_turned, p_wide, p_projected, p_placed = sem("p_turned"), sem("p_wide"), sem("p_projected"), sem("p_placed")
        top_placed, top_spread, bias_made, row_shifted = sem("top_placed"), sem("top_spread"), sem("bias_made"), sem("row_shifted")
        v_made, w_made, r_made, g_scaled = sem("v_made"), sem("w_made"), sem("r_made"), sem("g_scaled")
        mean_ready, mean_spread, mean_kept = sem("mean_ready"), sem("mean_spread"), sem("mean_kept")
        rq_ready, rows_spread, rows_kept = sem("rq_ready"), sem("rows_spread"), sem("rows_kept")
        mask_made, slot_used, e_made, e_used, deep_used = sem("mask_made"), sem("slot_used"), sem("e_made"), sem("e_used"), sem("deep_used")
        acc_summed = [sem(f"acc_summed{b}") for b in range(NB)]
        acc_taken = sem("acc_taken")
        post_done = sem("post_done")
        in_again, n_var, n_dev, n_scale, n_norm = sem("in_again"), sem("n_var"), sem("n_dev"), sem("n_scale"), sem("n_norm")
        n_turned, n_wide, ff_done, neg_made, exp_made = sem("n_turned"), sem("n_wide"), sem("ff_done"), sem("neg_made"), sem("exp_made")

        block = ctx.enter_context(nc.Block())

        def blocks(t, q, n=S, at=0):
            return t[:, bass.ds(q * S + at, n)] if not isinstance(q, int) else t[:, q * S + at:q * S + at + n]

        def span(t, start, n):
            return t[:, bass.ds(start, n)] if not isinstance(start, int) else t[:, start:start + n]

        def quarters(eng, turns, body, steps=None, per_turn=0, first=0):
            with eng.Fori(first, first + turns) as q:
                if steps:
                    steps.enter(q - first if first else q, per_turn)
                body(q)
            if steps:
                steps.leave(turns)

        def take_banks(b):
            return min(3, S - 3 * b)

        @block.sync
        def _(sp):
            for q in range(Q):
                sp.dma_start(X[:, q * S:(q + 1) * S, :],
                             x[q * QC:(q + 1) * QC, :].rearrange("(s p) d -> p s d", p=P)).then_inc(x_loaded, 16)
            loads = [(w0T, w0_t), (bias0_b, bias0.partition_broadcast(P)), (w2raw, w2_t),
                     (attnc[:, 0:4], attn),
                     (attnc[:, 4:6], a2),
                     (alphac, alpha.partition_broadcast(P)),
                     (dsub[:, :], diag)]
            for h in range(HEADS):
                loads += [(ff0raw[h], ff0[h]), (proj1[h][:, 0:D], ff0_t[h]), (ff1T[:, h, :], ff1_t[h])]
            for c, v in ((g1c, g1), (b1c, b1), (g2c, g2), (b2c, b2)):
                loads.append((c, v.rearrange("(c o) -> c o", o=1)))
            assert len(loads) == 17
            for dst, src in loads:
                sp.dma_start(dst, src).then_inc(weights_loaded, 16)

            def stream(src, ring_slots, loaded, used, q, run):
                L = len(loaded)
                for k in range(T):
                    if k >= L:
                        sp.wait_ge(used, q * (T - 1) + k - L + 1)
                    elif not isinstance(q, int):
                        if k == L - 1:
                            sp.wait_ge(acc_summed[NB - 1], q + run)
                        else:
                            sp.wait_ge(used, q * (T - 1) + k - L + 2)
                    sp.dma_start(ring_slots(k % L), span(src[k * P:(k + 1) * P, :], q * QC, QC))\
                        .then_inc(loaded[k % L], 16)

            def layer0(q):
                stream(adj_t, lambda s: ring[:, s, :], slot_loaded, slot_used, q, 0)

            layer0(0)
            quarters(sp, Q - 1, layer0, first=1)

            sp.wait_ge(post_done, RUNS2)
            sp.dma_start(proj2[:, 0:D], w2).then_inc(w2_loaded, 16)

            def layer3(q):
                stream(adj, lambda s: stream3[:, s, :], deep_loaded, deep_used, q, RUNS3)

            sp.wait_ge(e_made, 12 * T)
            layer3(0)
            quarters(sp, Q - 1, layer3, first=1)
            sp.wait_ge(stored, 16 * Q)

        @block.gpsimd
        def _(pool):
            nc.gpsimd.memset(ident[:, :], 0.0).then_inc(ident_zero, 1)
            pool.wait_ge(ident_zero, 1)
            nc.gpsimd.affine_select(out=ident[:, :], in_=ident[:, :], compare_op=ALU.not_equal, fill=1.0,
                                    base=0, pattern=[[-1, P]], channel_multiplier=1).then_inc(consts_made, 1)

        @block.tensor
        def _(pe):
            def products(n, k, lhs, g, done):
                for s in range(S):
                    b = s // 3
                    if k == 0 and s % 3 == 0 and not (isinstance(n, int) and n == 0):
                        pe.wait_ge(acc_taken, n * NB - NB + b + 1)
                    mm = pe.matmul(acc[:, b, (s % 3) * DW:(s % 3) * DW + DW], lhs[:, s * P:(s + 1) * P], g,
                                   start=(k == 0 and s % 3 == 0), stop=(k == T - 1), skip_group_check=True)
                    if k == T - 1 and (s % 3 == 2 or s == S - 1):
                        mm.then_inc(acc_summed[b], 1)
                    elif s == S - 1:
                        mm.then_inc(done, 1)

            def spread(col, dst):
                return pe.matmul(dst, col.broadcast_to([P, P]), ident[:, :], start=True, stop=True)

            def prologue(L, q):
                pq = L * Q + q
                pe.wait_ge(p_norm, pq + 1)
                if not (isinstance(pq, int) and pq == 0):
                    pe.wait_ge(p_wide, pq)
                for s in range(S):
                    mm = pe.transpose(turn[:, s * P:(s + 1) * P], V[:, s, :], ident[:, :])
                mm.then_inc(p_turned, 1)
                pe.wait_ge(p_wide, pq + 1)
                if not (isinstance(pq, int) and pq == 0):
                    pe.wait_ge(p_placed, pq)
                for h, (w, dst, width) in enumerate([[(w0T, acc, D)], [(proj1[0], acc, PW), (proj1[1], mix, PW)],
                                                     [(proj2, acc, PW)]][L]):
                    for s in range(S):
                        mm = pe.matmul(dst[:, s // 3, (s % 3) * PW:(s % 3) * PW + width],
                                       U[:, s * P:(s + 1) * P], w[:, 0:width], start=True, stop=True,
                                       skip_group_check=True)
                mm.then_inc(p_projected, 1)

            def spread_top(h):
                pe.wait_ge(top_placed, h + 1)
                spread(top, one).then_inc(top_spread, 1)

            def spread_rows(m):
                pe.wait_ge(rq_ready, m + 1)
                if not (isinstance(m, int) and m == 0):
                    pe.wait_ge(rows_kept, m)
                for s in range(S):
                    mm = spread(rq[:, s:s + 1], turn[:, s * P:(s + 1) * P])
                mm.then_inc(rows_spread, 1)

            def post1(j):
                def turns():
                    pe.wait_ge(n_norm, j + 1)
                    pe.wait_ge(rows_kept, j + 2)
                    for s in range(S):
                        mm = pe.transpose(turn[:, s * P:(s + 1) * P], V[:, s, :], ident[:, :])
                    mm.then_inc(n_turned, 1)

                def apply(h):
                    pe.wait_ge(n_wide, j + 1)
                    for s in range(S):
                        mm = pe.matmul(mixed[:, s * P:(s + 1) * P], U[:, s * P:(s + 1) * P], ff1T[:, h, :],
                                       start=True, stop=True, skip_group_check=True)
                    mm.then_inc(ff_done, 1)
                return turns, apply

            pe.wait_ge(consts_made, 1)
            pe.wait_ge(weights_loaded, 16 * 17)
            for h, raw in enumerate(ff0raw + [w2raw]):
                mm = pe.matmul(one[:, 2 * h:2 * h + 2], raw, attnc[:, 2 * h:2 * h + 2], start=True, stop=True,
                               skip_group_check=True)
            mm.then_inc(qv_summed, 1)

            quarters(pe, Q, lambda q: prologue(0, q))
            pe.wait_ge(p_placed, Q)

            def run0(q):
                for k in range(T):
                    pe.wait_ge(slot_loaded[k % STREAM], (q * (T // STREAM) + k // STREAM + 1) * 16)
                    pe.wait_ge(mask_made, q * T + k + 1)
                    products(q, k, ring[:, k % STREAM, :], G[:, 0, k, :], slot_used)
            run0(0)
            quarters(pe, Q - 1, run0, first=1)

            pe.wait_ge(acc_taken, RUNS1 * NB)
            pe.wait_ge(qv_placed, 1)
            quarters(pe, Q, lambda q: prologue(1, q))
            spread_top(0)
            spread_top(1)
            pe.wait_ge(p_wide, 2 * Q)
            spread_rows(0)

            def attention(m, g, hooks, guard):
                for k in range(T):
                    pe.wait_ge(e_made, m * T + k + 1)
                    if guard is not None and k % S == 0:
                        pe.wait_ge(g_scaled, guard + k // S + 1)
                    products(RUNS1 + m, k, E[k % 2], g[:, k, :], e_used)
                    if k in hooks:
                        hooks[k]()

            def layer1_run(h, q, post, last=False):
                m = q * HEADS + h
                hooks = {}
                if post is not None:
                    ph, j = post
                    turns, apply = post1(j)
                    hooks = {16: turns, 20: lambda: apply(ph)}
                if not last:
                    hooks[28] = lambda: spread_rows(m + 1)
                attention(m, G[:, h, :, :], hooks, h * Q)

            layer1_run(0, 0, None)

            def layer1_body(q):
                layer1_run(1, q, (0, q * HEADS))
                layer1_run(0, q + 1, (1, q * HEADS + 1))
            quarters(pe, Q - 1, layer1_body)
            layer1_run(1, Q - 1, (0, HEADS * (Q - 1)), last=True)
            j = HEADS * Q - 1
            pe.wait_ge(n_norm, j + 1)
            for s in range(S):
                mm = pe.transpose(turn[:, s * P:(s + 1) * P], V[:, s, :], ident[:, :])
            mm.then_inc(n_turned, 1)
            post1(j)[1](1)

            pe.wait_ge(acc_taken, RUNS2 * NB)
            pe.wait_ge(post_done, RUNS2)
            pe.wait_ge(qv2_placed, 1)
            quarters(pe, Q, lambda q: prologue(2, q))
            pe.wait_ge(mean_ready, 1)
            pe.matmul(mixed[:, 0:D], hmean.broadcast_to([P, P]), proj2[:, 0:D], start=True, stop=True)\
                .then_inc(mean_spread, 1)
            spread_top(2)
            spread_rows(HEADS * Q)
            for q in range(Q):
                m = HEADS * Q + q
                attention(m, G[:, 0, :, :],
                          {28: lambda m=m: spread_rows(m + 1)} if q < Q - 1 else {}, 2 * Q)

            def run3(q):
                for k in range(T):
                    pe.wait_ge(deep_loaded[k % DEEP], (q * (T // DEEP) + k // DEEP + 1) * 16)
                    if k % S == 0:
                        pe.wait_ge(p_norm, 3 * Q + k // S + 1)
                    products(RUNS3 + q, k, stream3[:, k % DEEP, :], G[:, 1, k, :], deep_used)
            run3(0)
            quarters(pe, Q - 1, run3, first=1)

        @block.scalar
        def _(act):
            st = Steps(act, act_step)

            def normalise(dst, src, mul, add, func, done):
                for s in range(S):
                    ins = act.activation(dst(s), src(s), func, bias=add(s), scale=mul(s))
                ins.then_inc(done, 1)

            def local(t):
                return lambda s: t[:, s:s + 1]

            def prologue(L, q):
                pq = L * Q + q
                act.wait_ge(p_var, pq + 1)
                act.activation(dev[:, :], var[:, :], ACT.Sqrt).then_inc(p_dev, 1)
                act.wait_ge(p_scale, pq + 1)
                if L == 3:
                    normalise(lambda s: blocks(G[:, 1, :, :], q, 1, s)[:, 0, 0:D], lambda s: blocks(X, q, 1, s)[:, 0, :],
                              local(scale), local(shift), ACT.Relu, p_norm)
                    return
                if not (isinstance(pq, int) and pq == 0):
                    act.wait_ge(p_turned, pq)
                normalise(lambda s: V[:, s, :], lambda s: blocks(X, q, 1, s)[:, 0, :],
                          local(scale), local(shift), ACT.Relu, p2_in if L == 1 else p_norm)
                if L == 1:
                    act.wait_ge(p2_var, q + 1)
                    act.activation(dev[:, :], var[:, :], ACT.Sqrt).then_inc(p2_dev, 1)
                    act.wait_ge(p2_scale, q + 1)
                    normalise(lambda s: V[:, s, :], lambda s: V[:, s, :], local(scale), local(shift),
                              ACT.Identity, p_norm)
                act.wait_ge(p_turned, pq + 1)
                if not (isinstance(pq, int) and pq == 0):
                    act.wait_ge(p_placed, pq)
                for c in range(2):
                    src, dst = turn[:, c * BANK:(c + 1) * BANK], U[:, c * BANK:(c + 1) * BANK]
                    if L == 1:
                        ins = act.activation(dst, src, ACT.Identity, bias=b1c, scale=g1c)
                    else:
                        ins = act.copy(dst, src)
                ins.then_inc(p_wide, 1)

            def exponentials(h, gslot):
                s_ = SLOPES[h]
                act.wait_ge(bias_made, h + 1)
                act.activation(G[:, gslot, :, D], rank[:, h, :], ACT.Exp, bias=vbias, scale=s_).then_inc(v_made, 1)
                act.wait_ge(v_made, h + 1)
                act.activation(rank[:, h, :], rank[:, h, :], ACT.Exp, bias=wbias, scale=1.0 - s_).then_inc(w_made, 1)
                act.wait_ge(row_shifted, h + 1)
                act.activation(row[:, h, :], row[:, h, :], ACT.Exp, scale=-(1.0 - s_)).then_inc(r_made, 1)

            def rows_columns(m, h, q):
                if isinstance(m, int) and m == 0:
                    act.wait_ge(r_made, HEADS)
                elif isinstance(m, int) and m == HEADS * Q:
                    act.wait_ge(r_made, 3)
                if not (isinstance(m, int) and m == 0):
                    act.wait_ge(rows_spread, m)
                act.copy(rq[:, :], blocks(row[:, h, :], q)).then_inc(rq_ready, 1)

            def rows_copy(m, slot):
                act.wait_ge(rows_spread, m + 1)
                if not (isinstance(m, int) and m < 2):
                    act.wait_ge(e_made, m * T - T)
                act.copy(R[slot][:, 0:BANK], turn[:, 0:BANK])
                act.copy(R[slot][:, BANK:2 * BANK], turn[:, BANK:2 * BANK]).then_inc(rows_kept, 1)

            def take(n):
                if not (isinstance(n, int) and n == 0):
                    act.wait_ge(post_done, n)
                for b in range(NB):
                    w = take_banks(b) * DW
                    act.wait_ge(acc_summed[b], n + 1)
                    act.copy(U[:, b * 3 * DW:b * 3 * DW + w], acc[:, b, 0:w]).then_inc(acc_taken, 1)

            def post1(h, q):
                j = q * HEADS + h
                n = RUNS1 + j

                def again():
                    take(n)
                    normalise(lambda s: V[:, s, :], lambda s: blocks(X, q, 1, s)[:, 0, :],
                              lambda s: blocks(norm_scale, q, 1, s), lambda s: blocks(norm_shift, q, 1, s),
                              ACT.Relu, in_again)

                def deviation():
                    act.wait_ge(n_var, j + 1)
                    act.activation(dev[:, :], var[:, :], ACT.Sqrt).then_inc(n_dev, 1)

                def norm():
                    act.wait_ge(n_scale, j + 1)
                    normalise(lambda s: V[:, s, :], lambda s: U3[:, s, 0:D], local(scale), local(shift),
                              ACT.Identity, n_norm)

                def widen():
                    act.wait_ge(n_turned, j + 1)
                    act.wait_ge(n_norm, j + 1)
                    for c in range(2):
                        ins = act.activation(U[:, c * BANK:(c + 1) * BANK], turn[:, c * BANK:(c + 1) * BANK],
                                             ACT.Identity, bias=b2c, scale=g2c)
                    ins.then_inc(n_wide, 1)

                def expo():
                    act.wait_ge(neg_made, j + 1)
                    act.activation(V[:, :, :], V[:, :, :], ACT.Exp).then_inc(exp_made, 1)
                return [again, deviation, norm, widen, expo]

            act.wait_ge(x_loaded, 16 * Q)
            quarters(act, Q, lambda q: prologue(0, q))
            act.wait_ge(p_projected, Q)
            take(0)
            quarters(act, Q - 1, take, first=1)

            act.wait_ge(post_done, RUNS1)
            act.wait_ge(weights_loaded, 16 * 17)
            quarters(act, Q, lambda q: prologue(1, q))
            exponentials(0, 0)
            exponentials(1, 1)
            rows_columns(0, 0, 0)
            rows_copy(0, 0)
            act.wait_ge(p_projected, 2 * Q)

            def next_rows(h, q):
                m = q * HEADS + h
                rows_columns(m, h, q)
                rows_copy(m, h)

            next_rows(1, 0)

            def layer1_body(q):
                for f in post1(0, q):
                    f()
                next_rows(0, q + 1)
                for f in post1(1, q):
                    f()
                next_rows(1, q + 1)
            quarters(act, Q - 1, layer1_body)
            for h in range(HEADS):
                for f in post1(h, Q - 1):
                    f()

            act.wait_ge(post_done, RUNS2)
            quarters(act, Q, lambda q: prologue(2, q))
            exponentials(2, 0)
            rows_columns(HEADS * Q, 2, 0)
            rows_copy(HEADS * Q, 0)
            act.wait_ge(p_projected, 3 * Q)
            for q in range(Q):
                if q < Q - 1:
                    m = HEADS * Q + q + 1
                    rows_columns(m, 2, q + 1)
                    rows_copy(m, (q + 1) % 2)
                take(RUNS2 + q)

            act.wait_ge(post_done, RUNS3)
            quarters(act, Q, lambda q: prologue(3, q))

            def store(q):
                take(RUNS3 + q)
                act.wait_ge(post_done, RUNS3 + q + 1)
                act.dma_start(span(out.rearrange("(t p) d -> p t d", p=P), q * S, S), V[:, :, :]).then_inc(stored, 16)
            quarters(act, Q, store)

        @block.vector
        def _(dve):
            st = Steps(dve, dve_step)
            V3 = V[:, :, :]
            Uf = U3[:, :, 0:D]
            Ud = U3[:, :, D]

            def wide(t):
                return t[:, :].unsqueeze(2).broadcast_to([P, S, D])

            def statistics(src, made):
                for s in range(S):
                    ins = dve.bn_stats(stats[:, s, :], src(s))
                st.then(ins)
                dve.tensor_tensor(twice, stats[:, :, 1], stats[:, :, 4], ALU.add)
                dve.tensor_tensor(apart, stats[:, :, 1], stats[:, :, 4], ALU.subtract)
                st.then(dve.tensor_tensor(squares, stats[:, :, 2], stats[:, :, 5], ALU.add))
                dve.tensor_scalar(mean[:, :], twice, 0.5, None, ALU.mult)
                dve.tensor_tensor(apart, apart, apart, ALU.mult)
                st.then(dve.tensor_scalar(squares, squares, 1.0 / D, EPS, ALU.mult, ALU.add))
                dve.scalar_tensor_tensor(var[:, :], apart, 0.25, squares, ALU.mult, ALU.add).then_inc(made, 1)

            def scales(got, n, done, keep=None):
                dve.wait_ge(got, n)
                st.then(dve.reciprocal(scale[:, :], dev[:, :]))
                if keep is not None:
                    st.mark(dve.tensor_copy(blocks(norm_scale, keep), scale[:, :]))
                ins = dve.scalar_tensor_tensor(shift[:, :], mean[:, :], -1.0, scale[:, :], ALU.mult, ALU.mult)
                if keep is not None:
                    st.then(ins)
                    ins = dve.tensor_copy(blocks(norm_shift, keep), shift[:, :])
                ins.then_inc(done, 1)

            def prologue(L, q):
                pq = L * Q + q
                if not (isinstance(pq, int) and pq == 0):
                    dve.wait_ge(p_norm, pq)
                statistics(lambda s: blocks(X, q, 1, s)[:, 0, :], p_var)
                scales(p_dev, pq + 1, p_scale, keep=q if L == 1 else None)
                if L == 3:
                    return
                if L == 1:
                    dve.wait_ge(p2_in, q + 1)
                    statistics(lambda s: V[:, s, :], p2_var)
                    scales(p2_dev, q + 1, p2_scale)
                if L == 2:
                    dve.wait_ge(p_wide, pq + 1)
                    st.mark(dve.reduce_sum(span(hsum, q, 1), U[:, 0:S * D], AX_X))
                dve.wait_ge(p_projected, pq + 1)
                heads = [[(0, 0, acc)], [(0, 0, acc), (1, 1, mix)], [(2, 0, acc)]][L]
                for h, g, src in heads:
                    for b in range(NB):
                        c = take_banks(b)
                        got = src[:, b, 0:c * PW].rearrange("p (s d) -> p s d", d=PW)
                        ins = dve.tensor_copy(blocks(G[:, g, :, :], q, c, 3 * b)[:, :, 0:D], got[:, :, 0:D])
                        if L > 0:
                            st.mark(dve.tensor_copy(blocks(rank[:, h, :], q, c, 3 * b), got[:, :, D]))
                            st.mark(dve.tensor_copy(blocks(row[:, h, :], q, c, 3 * b), got[:, :, D + 1]))
                        if (h, g, src) != heads[-1] or b < NB - 1:
                            st.mark(ins)
                    if h == heads[-1][0]:
                        ins.then_inc(p_placed, 1)

            def top_of(h):
                s_ = SLOPES[h]
                st.wait()
                dve.reduce_max(top, rank[:, h, :], AX_X).then_inc(top_placed, 1)
                dve.wait_ge(top_spread, h + 1)
                if h == 1:
                    dve.wait_ge(w_made, 1)
                st.then(dve.reduce_max(bigc, one, AX_X))
                st.mark(dve.tensor_scalar(vbias, bigc, -s_, None, ALU.mult))
                dve.tensor_scalar(wbias, bigc, -(1.0 - s_), None, ALU.mult).then_inc(bias_made, 1)
                dve.tensor_scalar(row[:, h, :], row[:, h, :], bigc, 0.0, ALU.add, ALU.max).then_inc(row_shifted, 1)

            def scale_g(h, g, part):
                if part == 0:
                    dve.wait_ge(v_made, h + 1)
                gp = G[:, g, part * S:(part + 1) * S, :]
                v = gp[:, :, D:D + 1].broadcast_to([P, S, D])
                dve.tensor_tensor(gp[:, :, 0:D], gp[:, :, 0:D], v, ALU.mult).then_inc(g_scaled, 1)

            def e_block(m, q, k, h, r):
                if k >= 2 or not (isinstance(m, int) and m == 0):
                    if k >= 2:
                        dve.wait_ge(e_used, m * (T - 1) + k - 1)
                    else:
                        dve.wait_ge(acc_summed[NB - 1], m + RUNS1) if k == 1 else dve.wait_ge(e_used, m * (T - 1))
                pattern = span(mask, q * QC + k * N, QC)
                dve.scalar_tensor_tensor(E[k % 2], R[r], rank[:, h, k:k + 1], pattern, ALU.max, ALU.mult)\
                    .then_inc(e_made, 1)

            def diagonal(q, s):
                return span(mask, q * (S * (N + P)) + s * (N + P), P)

            dve.wait_ge(weights_loaded, 16 * 17)
            st.mark(dve.memset(G[:, 0, :, D], 1.0))
            st.mark(dve.tensor_scalar(restc, alphac, -1.0, 1.0, ALU.mult, ALU.add))
            st.mark(dve.tensor_scalar(dsub[:, :], dsub[:, :], 0.0, -1.0, ALU.is_gt, ALU.add))
            dve.wait_ge(qv_summed, 1)
            st.then(dve.tensor_copy(qv, one[:, 0:6]))
            for h in range(HEADS):
                st.mark(dve.tensor_copy(proj1[h][:, D:D + 1], qv[:, 2 * h + 1:2 * h + 2]))
                ins = dve.tensor_copy(proj1[h][:, D + 1:D + 2], qv[:, 2 * h:2 * h + 1])
                st.mark(ins) if h == 0 else ins.then_inc(qv_placed, 1)

            dve.wait_ge(x_loaded, 16 * Q)
            quarters(dve, Q, lambda q: prologue(0, q), st, 6)
            dve.wait_ge(consts_made, 1)

            def masks(q, hooks):
                for k in range(T):
                    dve.wait_ge(slot_loaded[k % STREAM], (q * (T // STREAM) + k // STREAM + 1) * 16)
                    dve.tensor_scalar(span(mask, q * QC + k * N, QC), ring[:, k % STREAM, :], 0.0, None,
                                      ALU.is_gt).then_inc(mask_made, 1)
                    if k in hooks:
                        hooks[k]()

            def post0(q):
                def divisors():
                    dve.wait_ge(acc_taken, (q + 1) * NB)
                    st.then(dve.tensor_scalar(inv[:, :], Ud, alphac, restc, ALU.mult, ALU.add))
                    st.then(dve.tensor_scalar(zero[:, :], inv[:, :], 0.0, None, ALU.is_equal))
                    st.then(dve.tensor_tensor(inv[:, :], inv[:, :], zero[:, :], ALU.add))
                    st.then(dve.reciprocal(inv[:, :], inv[:, :]))
                    st.then(dve.tensor_scalar(zero[:, :], zero[:, :], -1.0, 1.0, ALU.mult, ALU.add))
                    st.then(dve.tensor_tensor(inv[:, :], inv[:, :], zero[:, :], ALU.mult))

                def own():
                    st.then(dve.tensor_scalar(V3, blocks(G[:, 0, :, :], q)[:, :, 0:D], restc, None, ALU.mult))
                    st.then(dve.scalar_tensor_tensor(Uf, Uf, alphac, V3, ALU.mult, ALU.add))

                def divide():
                    st.then(dve.tensor_tensor(Uf, Uf, wide(inv), ALU.mult))

                def bias():
                    st.then(dve.tensor_tensor(Uf, Uf, bias0_b.unsqueeze(1).broadcast_to([P, S, D]), ALU.add))

                def self_loops():
                    dve.wait_ge(mask_made, (q + 1) * T)
                    for s in range(S):
                        ins = dve.tensor_tensor(diagonal(q, s), diagonal(q, s), ident[:, :], ALU.max)
                    st.mark(ins)

                def add():
                    dve.scalar_tensor_tensor(blocks(X, q), Uf, 0.0, blocks(X, q), ALU.max, ALU.add)\
                        .then_inc(post_done, 1)
                return {2: divisors, 5: own, 8: divide, 11: bias, 14: self_loops, 17: add}

            masks(0, {})
            quarters(dve, Q - 1, lambda q: masks(q, post0(q - 1)), st, 11, first=1)
            for f in post0(Q - 1).values():
                f()

            dve.wait_ge(post_done, RUNS1)
            dve.wait_ge(acc_summed[NB - 1], RUNS1)
            st.wait()
            quarters(dve, Q, lambda q: prologue(1, q), st, 27)
            dve.wait_ge(p_placed, 2 * Q)
            top_of(0)
            top_of(1)
            for part in range(Q):
                scale_g(0, 0, part)

            def layer1_run(h, q, post, before=None):
                m = q * HEADS + h
                dve.wait_ge(rows_kept, m + 1)
                if isinstance(m, int) and m < 2:
                    dve.wait_ge(w_made, m + 1)
                for k in range(T):
                    e_block(m, q, k, h, h)
                    if post and k in post:
                        post[k]()

            def post1(h, q):
                j = q * HEADS + h
                n = RUNS1 + j

                def divide():
                    dve.wait_ge(acc_taken, (n + 1) * NB)
                    st.then(dve.reciprocal(inv[:, :], Ud))
                    st.mark(dve.tensor_tensor(Uf, Uf, wide(inv), ALU.mult))

                def residual():
                    dve.wait_ge(in_again, j + 1)
                    st.wait()
                    st.then(dve.tensor_tensor(Uf, Uf, V3, ALU.add))

                def stat():
                    statistics(lambda s: U3[:, s, 0:D], n_var)

                def scal():
                    scales(n_dev, j + 1, n_scale)

                def negative():
                    dve.wait_ge(ff_done, j + 1)
                    dve.tensor_scalar(V3, mixed3, 0.0, None, ALU.min).then_inc(neg_made, 1)

                def elu():
                    dve.wait_ge(exp_made, j + 1)
                    dst = elu0 if h == 0 else V3
                    ins = dve.scalar_tensor_tensor(dst, mixed3, 0.0, V3, ALU.max, ALU.add)
                    if h == 0:
                        ins.then_inc(post_done, 1)
                    else:
                        st.mark(ins)

                def add():
                    if h == 0:
                        return
                    st.wait()
                    st.then(dve.tensor_tensor(V3, V3, elu0, ALU.add))
                    st.then(dve.tensor_scalar(V3, V3, 1.0 / HEADS, -1.0, ALU.mult, ALU.add))
                    dve.tensor_tensor(blocks(X, q), blocks(X, q), V3, ALU.add).then_inc(post_done, 1)

                def own_pattern():
                    if h == 0:
                        return
                    dve.wait_ge(e_made, (j + 1) * T)
                    for s in range(S):
                        ins = dve.scalar_tensor_tensor(diagonal(q, s), ident[:, :], blocks(dsub, q, 1, s),
                                                       diagonal(q, s), ALU.mult, ALU.add)
                    st.mark(ins)
                return {2: divide, 5: residual, 7: stat, 11: scal, 14: own_pattern, 23: negative, 26: elu, 29: add}

            with_g = {6: lambda: scale_g(1, 1, 0), 8: lambda: scale_g(1, 1, 1), 10: lambda: scale_g(1, 1, 2),
                      12: lambda: scale_g(1, 1, 3)}
            layer1_run(0, 0, with_g)
            dve.wait_ge(w_made, HEADS)

            def layer1_body(q):
                layer1_run(1, q, post1(0, q))
                layer1_run(0, q + 1, post1(1, q))
            quarters(dve, Q - 1, layer1_body, st, 7 + 11)
            layer1_run(1, Q - 1, post1(0, Q - 1))
            for f in post1(1, Q - 1).values():
                f()

            dve.wait_ge(w2_loaded, 16)
            st.mark(dve.tensor_copy(proj2[:, D:D + 1], qv[:, 5:6]))
            dve.tensor_copy(proj2[:, D + 1:D + 2], qv[:, 4:5]).then_inc(qv2_placed, 1)
            dve.wait_ge(post_done, RUNS2)
            dve.wait_ge(acc_summed[NB - 1], RUNS2)
            quarters(dve, Q, lambda q: prologue(2, q), st, 13)
            dve.wait_ge(p_placed, 3 * Q)
            st.wait()
            st.then(dve.reduce_sum(hmean, hsum, AX_X))
            dve.tensor_scalar(hmean, hmean, 1.0 / N, None, ALU.mult).then_inc(mean_ready, 1)
            dve.wait_ge(mean_spread, 1)
            dve.tensor_copy(mean2, mixed[:, 0:D]).then_inc(mean_kept, 1)
            top_of(2)
            for part in range(Q):
                scale_g(2, 0, part)

            def post2(q):
                def divisors():
                    dve.wait_ge(acc_taken, (RUNS2 + q + 1) * NB)
                    st.then(dve.tensor_scalar(zero[:, :], Ud, 0.0, None, ALU.is_equal))
                    st.then(dve.tensor_tensor(inv[:, :], Ud, zero[:, :], ALU.add))
                    st.then(dve.reciprocal(inv[:, :], inv[:, :]))

                def divide():
                    st.mark(dve.tensor_tensor(Uf, Uf, wide(inv), ALU.mult))

                def lonely():
                    dve.wait_ge(mean_kept, 1)
                    st.then(dve.tensor_tensor(V3, mean2.unsqueeze(1).broadcast_to([P, S, D]), wide(zero), ALU.mult))
                    st.then(dve.tensor_tensor(Uf, Uf, V3, ALU.add))

                def add():
                    dve.scalar_tensor_tensor(blocks(X, q), Uf, 0.0, blocks(X, q), ALU.max, ALU.add)\
                        .then_inc(post_done, 1)
                return {2: divisors, 5: divide, 8: lonely, 12: add}

            for q in range(Q):
                m = HEADS * Q + q
                dve.wait_ge(rows_kept, m + 1)
                if q == 0:
                    dve.wait_ge(w_made, 3)
                hooks = post2(q - 1) if q else {}
                for k in range(T):
                    e_block(m, q, k, 2, q % 2)
                    if k in hooks:
                        hooks[k]()
                if q == 0:
                    st.mark(dve.memset(G[:, 1, :, D], 1.0))
            for f in post2(Q - 1).values():
                f()

            dve.wait_ge(post_done, RUNS3)
            quarters(dve, Q, lambda q: prologue(3, q), st, 4)

            def post3(q):
                dve.wait_ge(acc_taken, (RUNS3 + q + 1) * NB)
                st.then(dve.tensor_scalar(zero[:, :], Ud, 0.0, None, ALU.is_equal))
                st.then(dve.tensor_tensor(inv[:, :], Ud, zero[:, :], ALU.add))
                st.then(dve.reciprocal(inv[:, :], inv[:, :]))
                st.then(dve.tensor_scalar(zero[:, :], zero[:, :], -1.0, 1.0, ALU.mult, ALU.add))
                st.then(dve.tensor_tensor(inv[:, :], inv[:, :], zero[:, :], ALU.mult))
                st.then(dve.tensor_tensor(Uf, Uf, wide(inv), ALU.mult))
                if not isinstance(q, int):
                    dve.wait_ge(stored, q * 16)
                dve.tensor_tensor(V3, Uf, blocks(X, q), ALU.add).then_inc(post_done, 1)
            post3(0)
            quarters(dve, Q - 1, post3, st, 6, first=1)


def kernel(**inputs):
    import numpy as np
    import concourse.bacc as bacc
    from concourse.bass_utils import run_bass_kernel_spmd

    nc = bacc.Bacc("TRN2", target_bir_lowering=False, num_devices=1)
    g = {k: np.asarray(v) for k, v in inputs.items()}
    given = {
        "x": g["x"], "adj": g["adj"], "adj_t": g["adj"].T, "diag": g["adj"].diagonal().reshape(-1, P).T,
        "alpha": g["L0_gnn_alpha"],
        "w0_t": g["L0_gnn_W"].T, "bias0": g["L0_gnn_b"],
        "ff0": g["L1_gnn_ff0_w"], "ff0_t": g["L1_gnn_ff0_w"].transpose(0, 2, 1),
        "ff1_t": g["L1_gnn_ff1_w"].transpose(0, 2, 1), "attn": g["L1_gnn_attn_w"].reshape(4, P).T,
        "g1": g["L1_gnn_g1"], "b1": g["L1_gnn_b1"], "g2": g["L1_gnn_g2"], "b2": g["L1_gnn_b2"],
        "w2": g["L2_gnn_W"], "w2_t": g["L2_gnn_W"].T, "a2": g["L2_gnn_a"].reshape(2, P).T,
    }
    arrays, args = {}, []
    for name, a in given.items():
        a = np.ascontiguousarray(a)
        arrays[f"in_{name}"] = a
        args.append(nc.dram_tensor(f"in_{name}", a.shape, mybir.dt.from_np(a.dtype), kind="ExternalInput").ap())
    args.append(nc.dram_tensor("out_x", g["x"].shape, F32, kind="ExternalOutput").ap())
    graph_layers(nc, *args)
    r = run_bass_kernel_spmd(nc, [arrays], core_ids=[0])
    return r.results[0]["out_x"]
```

```python
from contextlib import ExitStack

import concourse.bass as bass
from concourse import mybir

P = 128
ALU = mybir.AluOpType
ACT = mybir.ActivationFunctionType
F32 = mybir.dt.float32
U8 = mybir.dt.uint8
AX_X = mybir.AxisListType.X
EPS = 1e-5


class Steps:

    def __init__(self, eng, sem):
        self.eng, self.sem, self.done, self.extra = eng, sem, 0, None

    def mark(self, ins):
        ins.then_inc(self.sem, 1)
        self.done += 1

    def wait(self):
        self.eng.wait_ge(self.sem, self.done if self.extra is None else self.extra + self.done)

    def then(self, ins):
        self.mark(ins)
        self.wait()

    def enter(self, turn, per_turn):
        self.start, self.per_turn, self.extra = self.done, per_turn, turn * per_turn

    def leave(self, turns):
        assert self.done - self.start == self.per_turn, (self.done - self.start, self.per_turn)
        self.done, self.extra = self.start + self.per_turn * turns, None


def graph_layers(nc, x, adj, adj_t, diag, alpha, w0_t, bias0, ff0, ff0_t, ff1_t, attn, g1, b1, g2, b2,
                 w2, w2_t, a2, out, kept0):
    N, D = x.shape
    T = N // P
    Q = 4
    S = T // Q
    QC = S * P
    DW = D + 1
    PW = D + 4
    HEADS = 2
    BANK = 512
    NB = (S + 2) // 3
    STREAM = 4
    DEEP = 8
    EB = 3
    WEIGHTS = 15

    with ExitStack() as ctx:
        def sb(name, shape, dt=F32):
            return ctx.enter_context(nc.sbuf_tensor(name, shape, dt))

        def sem(name):
            return ctx.enter_context(nc.semaphore(name))

        mask = sb("mask", [P, T * N], U8)
        X = sb("X", [P, T, D])
        G = sb("G", [P, 2, T, DW])
        ring = sb("ring", [P, 5, QC])
        U = sb("U", [P, S * DW])
        V = sb("V", [P, S, D])
        ident = sb("ident", [P, P])
        ff1T = sb("ff1T", [P, HEADS, D])
        score1 = sb("score1", [P, T, 4])
        score2 = sb("score2", [P, T, 2])
        norms = sb("norms", [P, 4, T])
        stats = sb("stats", [P, S, 6])
        mean = sb("mean", [P, S])
        parts = sb("parts", [P, 3, S])
        var = sb("var", [P, S])
        dev = sb("dev", [P, S])
        scale = sb("scale", [P, S])
        shift = sb("shift", [P, S])
        cols = sb("cols", [P, 32])
        rq = sb("rq", [P, S])
        inv = sb("inv", [P, S])
        zero = sb("zero", [P, S])
        dsub = sb("dsub", [P, T])

        E = [ring[:, i, :] for i in range(EB)]
        R = ring[:, 3, :]
        spare = ring[:, 4, :]
        w0T = spare[:, 0:D]
        bias0_b = spare[:, D:2 * D]
        proj1 = spare[:, 2 * D:2 * D + PW]
        o = 2 * D + PW
        ff0T1 = spare[:, o:o + D]
        ff0raw = [spare[:, o + (1 + h) * D:o + (2 + h) * D] for h in range(HEADS)]
        w2raw = spare[:, o + 3 * D:o + 4 * D]
        proj2 = spare[:, o + D:o + 2 * D + 2]
        mean2 = spare[:, o + 2 * D + 2:o + 3 * D + 2]
        stream3 = mask[:, 0:DEEP * QC * 4].bitcast(F32).rearrange("p (s c) -> p s c", c=QC)
        U3 = U[:, :].rearrange("p (s d) -> p s d", d=DW)
        flat = U[:, 0:S * D]
        kept = flat.rearrange("p (s d) -> p s d", d=D)
        g1c, b1c, g2c, b2c, alphac, restc, top, bigc, wbias, vbias = [cols[:, i:i + 1] for i in range(10)]
        twice, apart, squares = [parts[:, i, :] for i in range(3)]
        attnc = cols[:, 10:16]
        qv = cols[:, 16:22]
        hpart = [cols[:, 22 + c:23 + c] for c in range(2)]
        hmean = cols[:, 24:25]
        seen = cols[:, 25:26]

        acc = ctx.enter_context(nc.psum_tensor("acc", [P, NB, BANK], F32))
        turn = ctx.enter_context(nc.psum_tensor("turn", [P, 2 * BANK], F32))
        mix = ctx.enter_context(nc.psum_tensor("mix", [P, NB, BANK], F32))
        mixed = mix[:, 0:2, :].rearrange("p b c -> p (b c)")
        mixed3 = mixed.rearrange("p (s d) -> p s d", d=D)
        one = mix[:, 2, 0:P]

        SLOPE = {1: 0.01, 2: 0.01, 3: 0.2}
        rank = {1: score1[:, :, 0], 2: score1[:, :, 1], 3: score2[:, :, 0]}
        row = {1: score1[:, :, 2], 2: score1[:, :, 3], 3: score2[:, :, 1]}

        x_loaded = [sem(f"x_loaded{q}") for q in range(Q)]
        w0_loaded, weights_loaded, w2_loaded = sem("w0_loaded"), sem("weights_loaded"), sem("w2_loaded")
        saved, back, stored = sem("saved"), sem("back"), sem("stored")
        slot_loaded = [sem(f"slot_loaded{i}") for i in range(STREAM)]
        deep_loaded = [sem(f"deep_loaded{i}") for i in range(DEEP)]
        consts_made, ident_zero, dve_step = sem("consts_made"), sem("ident_zero"), sem("dve_step")
        qv_summed, qv_placed, qv2_placed = sem("qv_summed"), sem("qv_placed"), sem("qv2_placed")
        f_var, f_dev, f_scale, f_norm = sem("f_var"), sem("f_dev"), sem("f_scale"), sem("f_norm")
        f2_var, f2_dev, f2_scale, f2_in = sem("f2_var"), sem("f2_dev"), sem("f2_scale"), sem("f2_in")
        f_turned, f_wide, f_projected, f_placed = sem("f_turned"), sem("f_wide"), sem("f_projected"), sem("f_placed")
        top_placed, top_spread, bias_made, row_shifted = sem("top_placed"), sem("top_spread"), sem("bias_made"), sem("row_shifted")
        v_made, w_made, r_made, g_scaled = sem("v_made"), sem("w_made"), sem("r_made"), sem("g_scaled")
        half_summed, mean_ready, mean_spread, mean_kept = sem("half_summed"), sem("mean_ready"), sem("mean_spread"), sem("mean_kept")
        rq_ready, rows_spread, rows_kept = sem("rq_ready"), sem("rows_spread"), sem("rows_kept")
        mask_made, slot_used, e_made, e_used, deep_used = sem("mask_made"), sem("slot_used"), sem("e_made"), sem("e_used"), sem("deep_used")
        acc_summed = [sem(f"acc_summed{b}") for b in range(NB)]
        acc_taken = sem("acc_taken")
        post_done = sem("post_done")
        in_again, n_var, n_dev, n_scale, n_norm = sem("in_again"), sem("n_var"), sem("n_dev"), sem("n_scale"), sem("n_norm")
        n_turned, n_wide, ff_done, exp_made, half_made = sem("n_turned"), sem("n_wide"), sem("ff_done"), sem("exp_made"), sem("half_made")

        block = ctx.enter_context(nc.Block())

        def fixed(v):
            return isinstance(v, int)

        def span(t, start, n):
            return t[:, start:start + n] if fixed(start) else t[:, bass.ds(start, n)]

        def blocks(t, q, n=S, at=0):
            return span(t, q * S + at, n)

        def width(b):
            return min(3, S - 3 * b)

        def quarters(eng, first, last, body, steps=None, per_turn=0):
            with eng.Fori(first, last + 1) as q:
                if steps:
                    steps.enter(q - first if first else q, per_turn)
                body(q)
            if steps:
                steps.leave(last + 1 - first)

        def wait(eng, signal, count):
            if not fixed(count) or count > 0:
                eng.wait_ge(signal, count)

        @block.sync
        def _(sp):
            def load_x(q):
                sp.dma_start(X[:, q * S:(q + 1) * S, :],
                             x[q * QC:(q + 1) * QC, :].rearrange("(s p) d -> p s d", p=P)).then_inc(x_loaded[q], 16)

            def stream(src, slots, loaded, used, h, q, some=range(T)):
                L = len(loaded)
                for k in some:
                    if k >= L:
                        sp.wait_ge(used, q * (T - 1) + k - L + 1)
                    elif not fixed(q) and k == L - 1:
                        sp.wait_ge(acc_summed[NB - 1], q + h * Q)
                    elif not fixed(q):
                        sp.wait_ge(used, q * (T - 1) + k - L + 2)
                    sp.dma_start(slots(k % L), span(src[k * P:(k + 1) * P, :], q * QC, QC))\
                        .then_inc(loaded[k % L], 16)

            def layer0(q, some=range(T)):
                stream(adj_t, lambda s: ring[:, s, :], slot_loaded, slot_used, 0, q, some)

            def layer3(q):
                stream(adj, lambda s: stream3[:, s, :], deep_loaded, deep_used, 4, q)

            load_x(0)
            sp.dma_start(w0T, w0_t).then_inc(w0_loaded, 16)
            layer0(0, range(2))
            load_x(1)
            layer0(0, range(2, STREAM))
            load_x(2)
            load_x(3)
            loads = [(bias0_b, bias0.partition_broadcast(P)), (alphac, alpha.partition_broadcast(P)),
                     (w2raw, w2_t), (attnc[:, 0:4], attn), (attnc[:, 4:6], a2), (dsub[:, :], diag),
                     (proj1[:, 0:D], ff0_t[0]), (ff0T1, ff0_t[1])]
            loads += [(ff0raw[h], ff0[h]) for h in range(HEADS)]
            loads += [(c, v.rearrange("(c o) -> c o", o=1)) for c, v in ((g1c, g1), (b1c, b1), (g2c, g2), (b2c, b2))]
            loads += [(ff1T[:, :, :], ff1_t.rearrange("h c o -> c h o"))]
            assert len(loads) == WEIGHTS
            for dst, src in loads:
                sp.dma_start(dst, src).then_inc(weights_loaded, 16)
            layer0(0, range(STREAM, T))
            quarters(sp, 1, Q - 1, layer0)

            sp.wait_ge(qv_summed, 1)
            sp.dma_start(proj2[:, 0:D], w2).then_inc(w2_loaded, 16)

            sp.wait_ge(saved, 16 * Q)

            def bring_back(q):
                sp.wait_ge(ff_done, q + Q + 1)
                sp.dma_start(flat, span(kept0, q * QC, QC)).then_inc(back, 16)
            quarters(sp, 0, Q - 1, bring_back)

            sp.wait_ge(e_made, 3 * Q * T)
            layer3(0)
            quarters(sp, 1, Q - 1, layer3)
            sp.wait_ge(stored, 16 * Q)

        @block.gpsimd
        def _(pool):
            nc.gpsimd.memset(ident[:, :], 0.0).then_inc(ident_zero, 1)
            pool.wait_ge(ident_zero, 1)
            nc.gpsimd.affine_select(out=ident[:, :], in_=ident[:, :], compare_op=ALU.not_equal, fill=1.0,
                                    base=0, pattern=[[-1, P]], channel_multiplier=1).then_inc(consts_made, 1)

        @block.tensor
        def _(pe):
            def products(n, k, lhs, g, done):
                for s in range(S):
                    b = s // 3
                    if k == 0 and s % 3 == 0:
                        wait(pe, acc_taken, n * NB - NB + b + 1 if not (fixed(n) and n == 0) else 0)
                    mm = pe.matmul(acc[:, b, (s % 3) * DW:(s % 3) * DW + DW], lhs[:, s * P:(s + 1) * P], g,
                                   start=(k == 0 and s % 3 == 0), stop=(k == T - 1), skip_group_check=True)
                    if k == T - 1 and (s % 3 == 2 or s == S - 1):
                        mm.then_inc(acc_summed[b], 1)
                    elif s == S - 1:
                        mm.then_inc(done, 1)

            def spread(col, dst):
                return pe.matmul(dst, col.broadcast_to([P, P]), ident[:, :], start=True, stop=True)

            def turn_v():
                for s in range(S):
                    mm = pe.transpose(turn[:, s * P:(s + 1) * P], V[:, s, :], ident[:, :])
                return mm

            def feed(p, weights, wide, spreads, posts):
                def turned():
                    pe.wait_ge(f_norm, p + 1)
                    wait(pe, rows_kept, spreads)
                    turn_v().then_inc(f_turned, 1)

                def project():
                    pe.wait_ge(f_wide, p + 1)
                    wait(pe, f_placed, p)
                    wait(pe, post_done, posts)
                    for s in range(S):
                        mm = pe.matmul(mix[:, s // 3, (s % 3) * PW:(s % 3) * PW + wide],
                                       U[:, s * P:(s + 1) * P], weights, start=True, stop=True,
                                       skip_group_check=True)
                    mm.then_inc(f_projected, 1)
                return turned, project

            def post1(j, spreads, feeds):
                def turned():
                    pe.wait_ge(n_norm, j + 1)
                    pe.wait_ge(rows_kept, spreads)
                    turn_v().then_inc(n_turned, 1)

                def apply(h):
                    pe.wait_ge(n_wide, j + 1)
                    pe.wait_ge(f_placed, feeds)
                    for s in range(S):
                        mm = pe.matmul(mixed[:, s * P:(s + 1) * P], U[:, s * P:(s + 1) * P], ff1T[:, h, :],
                                       start=True, stop=True, skip_group_check=True)
                    mm.then_inc(ff_done, 1)
                return turned, apply

            def spread_top(i):
                pe.wait_ge(top_placed, i)
                spread(top, one).then_inc(top_spread, 1)

            def spread_rows(m):
                pe.wait_ge(rq_ready, m + 1)
                wait(pe, rows_kept, m)
                for s in range(S):
                    mm = spread(rq[:, s:s + 1], turn[:, s * P:(s + 1) * P])
                mm.then_inc(rows_spread, 1)

            def run(h, q, hooks):
                n = q + h * Q
                for k in range(T):
                    if h == 0:
                        pe.wait_ge(slot_loaded[k % STREAM], (q * (T // STREAM) + k // STREAM + 1) * 16)
                        pe.wait_ge(mask_made, q * T + k + 1)
                        if fixed(q) and q == 0 and k % S == 0:
                            pe.wait_ge(f_placed, k // S + 1)
                        lhs, used = ring[:, k % STREAM, :], slot_used
                    elif h == 4:
                        pe.wait_ge(deep_loaded[k % DEEP], (q * (T // DEEP) + k // DEEP + 1) * 16)
                        if fixed(q) and q == 0 and k % S == 0:
                            pe.wait_ge(f_norm, 4 * Q + k // S + 1)
                        lhs, used = stream3[:, k % DEEP, :], deep_used
                    else:
                        pe.wait_ge(e_made, (n - Q) * T + k + 1)
                        if fixed(q) and q == 0 and k % S == 0:
                            pe.wait_ge(g_scaled, (h - 1) * Q + k // S + 1)
                        lhs, used = E[k % EB], e_used
                    products(n, k, lhs, G[:, h % 2, k, :], used)
                    if k in hooks:
                        hooks[k]()

            pe.wait_ge(consts_made, 1)
            pe.wait_ge(w0_loaded, 16)
            own = [feed(p, w0T, D, 0, 0) for p in range(Q)]
            own[0][0]()
            own[0][1]()

            def scores_behind_projections():
                pe.wait_ge(weights_loaded, 16 * WEIGHTS)
                pe.wait_ge(f_placed, Q)
                for h, raw in enumerate(ff0raw + [w2raw]):
                    mm = pe.matmul(one[:, 2 * h:2 * h + 2], raw, attnc[:, 2 * h:2 * h + 2], start=True, stop=True,
                                   skip_group_check=True)
                mm.then_inc(qv_summed, 1)
            run(0, 0, {2: own[1][0], 4: own[1][1], 9: own[2][0], 12: own[2][1], 17: own[3][0], 20: own[3][1],
                       28: scores_behind_projections})

            def stage0(q):
                turned, project = feed(Q + q - 1, proj1, PW, 0, q)
                run(0, q, {20: turned, 23: project})
            pe.wait_ge(qv_placed, 1)
            quarters(pe, 1, Q - 1, stage0)
            for step in feed(2 * Q - 1, proj1, PW, 0, Q):
                step()
            spread_top(1)
            spread_top(2)
            spread_rows(0)

            def stage1(q):
                m = q
                turned, project = feed(q + 2 * Q, ff0T1, D, m + 1, q + Q)
                hooks = {23: turned, 26: project, 29: lambda: spread_rows(m + 1)}
                if not (fixed(q) and q == 0):
                    rows_turned, apply = post1(q - 1, m + 1, q + 2 * Q)
                    hooks.update({11: rows_turned, 13: lambda: apply(0)})
                run(1, q, hooks)
            stage1(0)
            quarters(pe, 1, Q - 1, stage1)

            def stage2(q, rows=True):
                m = q + Q
                first = fixed(q) and q == 0
                rows_turned, apply = post1(q - 1 + Q, m + 1, 3 * Q if first else q - 1 + 3 * Q)
                hooks = {11: rows_turned, 13: lambda: apply(0 if first else 1)}
                if not first:
                    turned, project = feed(q - 1 + 3 * Q, proj2, D + 2, m + 1, q + 2 * Q)
                    hooks.update({25: turned, 28: project})
                if rows:
                    hooks[30] = lambda: spread_rows(m + 1)
                run(2, q, hooks)
            stage2(0)
            pe.wait_ge(qv2_placed, 1)
            quarters(pe, 1, Q - 2, stage2)
            stage2(Q - 1, rows=False)
            rows_turned, apply = post1(2 * Q - 1, 2 * Q, 4 * Q - 1)
            rows_turned()
            apply(1)
            for step in feed(4 * Q - 1, proj2, D + 2, 2 * Q, 3 * Q):
                step()
            pe.wait_ge(mean_ready, 1)
            pe.wait_ge(f_placed, 4 * Q)
            pe.matmul(mixed[:, 0:D], hmean.broadcast_to([P, P]), proj2[:, 0:D], start=True, stop=True)\
                .then_inc(mean_spread, 1)
            spread_top(3)
            spread_rows(2 * Q)

            def stage3(q):
                m = q + 2 * Q
                run(3, q, {29: lambda: spread_rows(m + 1)})
            stage3(0)
            quarters(pe, 1, Q - 2, stage3)
            run(3, Q - 1, {})

            run(4, 0, {})
            quarters(pe, 1, Q - 1, lambda q: run(4, q, {}))

        @block.scalar
        def _(act):
            def settle():
                act.copy(seen, ident[:, 0:1])

            def normalise(dst, src, mul, add, func, done):
                for s in range(S):
                    ins = act.activation(dst(s), src(s), func, bias=add(s), scale=mul(s))
                if done is not None:
                    ins.then_inc(done, 1)

            def local(t):
                return lambda s: t[:, s:s + 1]

            def of_v(s):
                return V[:, s, :]

            def deviation(got, n, done):
                act.wait_ge(got, n)
                act.activation(dev[:, :], var[:, :], ACT.Sqrt).then_inc(done, 1)

            def widen(got, n, done, scale_=None, bias_=None, halves=None):
                act.wait_ge(got, n)
                for c in range(2):
                    src, dst = turn[:, c * BANK:(c + 1) * BANK], U[:, c * BANK:(c + 1) * BANK]
                    if halves is not None:
                        ins = act.activation(dst, src, ACT.Identity, accum_out=hpart[c])
                    elif scale_ is not None:
                        ins = act.activation(dst, src, ACT.Identity, bias=bias_, scale=scale_)
                    else:
                        ins = act.copy(dst, src)
                ins.then_inc(done, 1)

            def feed(h, p, q, posts=0):
                def of_x(s):
                    return blocks(X, q, 1, s)[:, 0, :]
                if h == 2:
                    act.wait_ge(rows_kept, 1)
                    def known(i):
                        return lambda s: blocks(norms[:, i, :], q, 1, s)
                    wait(act, saved, 0 if fixed(q) and q == 0 else q * 16)
                    settle()
                    normalise(of_v, of_x, known(0), known(1), ACT.Relu, f2_in)
                    act.wait_ge(f2_in, q + Q + 1)
                    normalise(of_v, of_v, known(2), known(3), ACT.Identity, f_norm)
                else:
                    deviation(f_var, p - Q + 1 if h > 2 else p + 1, f_dev)
                    act.wait_ge(f_scale, p - Q + 1 if h > 2 else p + 1)
                    settle()
                    if h == 4:
                        normalise(lambda s: blocks(G[:, 0, :, :], q, 1, s)[:, 0, 0:D], of_x, local(scale), local(shift),
                                  ACT.Relu, f_norm)
                        return
                    normalise(of_v, of_x, local(scale), local(shift), ACT.Relu, f2_in if h == 1 else f_norm)
                    if h == 1:
                        deviation(f2_var, q + 1, f2_dev)
                        act.wait_ge(f2_scale, q + 1)
                        normalise(of_v, of_v, local(scale), local(shift), ACT.Identity, f_norm)
                if h in (1, 2):
                    widen(f_turned, p + 1, f_wide, g1c, b1c)
                elif h == 3:
                    wait(act, half_summed, 0 if fixed(q) and q == 0 else q * 1)
                    widen(f_turned, p + 1, f_wide, halves=True)
                else:
                    widen(f_turned, p + 1, f_wide)
                act.wait_ge(f_projected, p + 1)
                for b in range(NB):
                    c = width(b)
                    got = mix[:, b, 0:c * PW].rearrange("p (s d) -> p s d", d=PW)
                    ins = act.copy(blocks(G[:, h % 2, :, :], q, c, 3 * b)[:, :, 0:D], got[:, :, 0:D])
                    if h == 1:
                        ins = act.copy(blocks(score1, q, c, 3 * b), got[:, :, D:D + 4])
                    if h == 3:
                        ins = act.copy(blocks(score2, q, c, 3 * b), got[:, :, D:D + 2])
                ins.then_inc(f_placed, 1)

            def exponentials(h):
                s_ = SLOPE[h]
                act.wait_ge(bias_made, h)
                act.activation(G[:, h % 2, :, D], rank[h], ACT.Exp, bias=vbias, scale=s_).then_inc(v_made, 1)
                act.activation(rank[h], rank[h], ACT.Exp, bias=wbias, scale=1.0 - s_).then_inc(w_made, 1)
                act.wait_ge(row_shifted, h)
                act.activation(row[h], row[h], ACT.Exp, scale=-(1.0 - s_)).then_inc(r_made, 1)

            def rows_columns(m, h, q):
                if fixed(q) and q == 0:
                    act.wait_ge(r_made, h)
                wait(act, rows_spread, m)
                act.copy(rq[:, :], blocks(row[h], q)).then_inc(rq_ready, 1)

            def rows_copy(m):
                act.wait_ge(rows_spread, m + 1)
                wait(act, e_made, m * T)
                act.copy(R[:, 0:BANK], turn[:, 0:BANK])
                act.copy(R[:, BANK:2 * BANK], turn[:, BANK:2 * BANK]).then_inc(rows_kept, 1)

            def next_rows(h, q):
                m = q + (h - 1) * Q
                rows_columns(m, h, q)
                rows_copy(m)

            def take(n):
                wait(act, post_done, n)
                for b in range(NB):
                    w = width(b) * DW
                    act.wait_ge(acc_summed[b], n + 1)
                    act.copy(U[:, b * 3 * DW:b * 3 * DW + w], acc[:, b, 0:w]).then_inc(acc_taken, 1)

            def post1(h, q):
                j = q + h * Q
                take(j + Q)
                normalise(of_v, lambda s: blocks(X, q, 1, s)[:, 0, :],
                          lambda s: blocks(norms[:, 0, :], q, 1, s), lambda s: blocks(norms[:, 1, :], q, 1, s),
                          ACT.Relu, in_again)
                deviation(n_var, j + 1, n_dev)
                act.wait_ge(n_scale, j + 1)
                normalise(of_v, lambda s: U3[:, s, 0:D], local(scale), local(shift), ACT.Identity, n_norm)
                act.wait_ge(n_norm, j + 1)
                widen(n_turned, j + 1, n_wide, g2c, b2c)
                act.wait_ge(ff_done, j + 1)
                act.activation(V[:, :, :], mixed3, ACT.Exp)
                act.activation(mixed3, mixed3, ACT.Relu).then_inc(exp_made, 1)
                if h == 0:
                    act.wait_ge(post_done, j + Q + 1)
                    act.activation(V[:, :, :], V[:, :, :], ACT.Copy, bias=-1.0, scale=1.0 / HEADS).then_inc(half_made, 1)
                    act.wait_ge(half_made, q + 1)
                    act.dma_start(span(kept0, q * QC, QC), V[:, :, :].rearrange("p s d -> p (s d)")).then_inc(saved, 16)

            act.wait_ge(consts_made, 1)
            for q in range(Q):
                act.wait_ge(x_loaded[q], 16)
                feed(0, q, q)

            def stage0(q):
                take(q - 1)
                act.wait_ge(post_done, q)
                feed(1, q - 1 + Q, q - 1)
            act.wait_ge(weights_loaded, 16 * WEIGHTS)
            quarters(act, 1, Q - 1, stage0)
            take(Q - 1)
            act.wait_ge(post_done, Q)
            feed(1, 2 * Q - 1, Q - 1)
            exponentials(1)
            exponentials(2)
            next_rows(1, 0)

            feed(2, 2 * Q, 0)
            next_rows(1, 1)

            def stage1(q):
                post1(0, q - 1)
                feed(2, q + 2 * Q, q)
                next_rows(1, q + 1)
            quarters(act, 1, Q - 2, stage1)
            post1(0, Q - 2)
            feed(2, 3 * Q - 1, Q - 1)
            next_rows(2, 0)

            post1(0, Q - 1)
            next_rows(2, 1)

            def stage2(q, rows=True):
                post1(1, q - 1)
                act.wait_ge(post_done, q + 2 * Q)
                feed(3, q - 1 + 3 * Q, q - 1)
                if rows:
                    next_rows(2, q + 1)
            act.wait_ge(saved, 16 * Q)
            quarters(act, 1, Q - 2, stage2)
            stage2(Q - 1, rows=False)
            stage2(Q, rows=False)
            exponentials(3)
            next_rows(3, 0)

            next_rows(3, 1)

            def stage3(q, rows=True):
                take(q - 1 + 3 * Q)
                act.wait_ge(post_done, q + 3 * Q)
                feed(4, q - 1 + 4 * Q, q - 1)
                if rows:
                    next_rows(3, q + 1)
            quarters(act, 1, Q - 2, stage3)
            stage3(Q - 1, rows=False)
            stage3(Q, rows=False)

            def store(q):
                take(q + 4 * Q)
                act.wait_ge(post_done, q + 4 * Q + 1)
                act.dma_start(span(out.rearrange("(t p) d -> p t d", p=P), q * S, S), V[:, :, :]).then_inc(stored, 16)
            quarters(act, 0, Q - 1, store)

        @block.vector
        def _(dve):
            st = Steps(dve, dve_step)
            V3 = V[:, :, :]
            Uf = U3[:, :, 0:D]
            Ud = U3[:, :, D]

            def wide(t):
                return t[:, :].unsqueeze(2).broadcast_to([P, S, D])

            def statistics(src, made):
                for s in range(S):
                    ins = dve.bn_stats(stats[:, s, :], src(s))
                st.then(ins)
                dve.tensor_tensor(twice, stats[:, :, 1], stats[:, :, 4], ALU.add)
                dve.tensor_tensor(apart, stats[:, :, 1], stats[:, :, 4], ALU.subtract)
                st.then(dve.tensor_tensor(squares, stats[:, :, 2], stats[:, :, 5], ALU.add))
                dve.tensor_scalar(mean[:, :], twice, 0.5, None, ALU.mult)
                dve.tensor_tensor(apart, apart, apart, ALU.mult)
                st.then(dve.tensor_scalar(squares, squares, 1.0 / D, EPS, ALU.mult, ALU.add))
                dve.scalar_tensor_tensor(var[:, :], apart, 0.25, squares, ALU.mult, ALU.add).then_inc(made, 1)

            def scales(got, n, done, keep=None):
                dve.wait_ge(got, n)
                st.then(dve.reciprocal(scale[:, :], dev[:, :]))
                if keep is not None:
                    i, q = keep
                    st.mark(dve.tensor_copy(blocks(norms[:, i, :], q), scale[:, :]))
                ins = dve.scalar_tensor_tensor(shift[:, :], mean[:, :], -1.0, scale[:, :], ALU.mult, ALU.mult)
                if keep is not None:
                    st.then(ins)
                    ins = dve.tensor_copy(blocks(norms[:, i + 1, :], q), shift[:, :])
                ins.then_inc(done, 1)

            def feed(h, p, q):
                c = p - Q + 1 if h > 2 else p + 1

                def first():
                    statistics(lambda s: blocks(X, q, 1, s)[:, 0, :], f_var)

                def first_scales():
                    wait(dve, f_norm, p)
                    scales(f_dev, c, f_scale, keep=(0, q) if h == 1 else None)

                def second():
                    dve.wait_ge(f2_in, q + 1)
                    statistics(of_v, f2_var)

                def second_scales():
                    scales(f2_dev, q + 1, f2_scale, keep=(2, q))

                def halves():
                    dve.wait_ge(f_wide, p + 1)
                    wait(dve, half_summed, 0 if fixed(q) and q == 0 else q * 1)
                    dve.scalar_tensor_tensor(hmean, hpart[0], hpart[1], hmean, ALU.add, ALU.add).then_inc(half_summed, 1)
                steps = [first, first_scales]
                if h == 1:
                    steps += [second, second_scales]
                if h == 3:
                    steps += [halves]
                return steps

            def of_v(s):
                return V[:, s, :]

            def top_of(h):
                s_ = SLOPE[h]
                dve.reduce_max(top, rank[h], AX_X).then_inc(top_placed, 1)
                dve.wait_ge(top_spread, h)
                wait(dve, w_made, h - 1)
                st.then(dve.reduce_max(bigc, one, AX_X))
                dve.tensor_scalar(vbias, bigc, -s_, None, ALU.mult)
                dve.tensor_scalar(wbias, bigc, -(1.0 - s_), None, ALU.mult).then_inc(bias_made, 1)
                dve.tensor_scalar(row[h], row[h], bigc, 0.0, ALU.add, ALU.max).then_inc(row_shifted, 1)

            def scale_g(h, part):
                if part == 0:
                    dve.wait_ge(v_made, h)
                gp = G[:, h % 2, part * S:(part + 1) * S, :]
                v = gp[:, :, D:D + 1].broadcast_to([P, S, D])
                dve.tensor_tensor(gp[:, :, 0:D], gp[:, :, 0:D], v, ALU.mult).then_inc(g_scaled, 1)

            def run(h, q, hooks):
                m = q + (h - 1) * Q
                dve.wait_ge(rows_kept, m + 1)
                if fixed(q) and q == 0:
                    dve.wait_ge(w_made, h)
                for k in range(T):
                    if k >= EB:
                        dve.wait_ge(e_used, m * (T - 1) + k - EB + 1)
                    elif k == 0:
                        wait(dve, e_used, m * (T - 1))
                    elif k == 1:
                        dve.wait_ge(acc_summed[NB - 1], m + Q)
                    dve.scalar_tensor_tensor(E[k % EB], R, rank[h][:, k:k + 1], span(mask, q * QC + k * N, QC),
                                             ALU.max, ALU.mult).then_inc(e_made, 1)
                    if k in hooks:
                        hooks[k]()

            def diagonal(q, s):
                return span(mask, q * (S * (N + P)) + s * (N + P), P)

            def at(ks, steps):
                assert len(ks) == len(steps)
                return dict(zip(ks, steps))

            for i in range(2):
                dve.memset(G[:, i, :, D], 1.0)
            st.mark(dve.memset(hmean, 0.0))
            own = [feed(0, p, p) for p in range(Q)]
            dve.wait_ge(x_loaded[0], 16)
            for step in own[0]:
                step()
            for q in range(1, Q):
                dve.wait_ge(x_loaded[q], 16)

            def masks(q, hooks):
                for k in range(T):
                    dve.wait_ge(slot_loaded[k % STREAM], (q * (T // STREAM) + k // STREAM + 1) * 16)
                    dve.tensor_scalar(span(mask, q * QC + k * N, QC), ring[:, k % STREAM, :], 0.0, None,
                                      ALU.is_gt).then_inc(mask_made, 1)
                    if k in hooks:
                        hooks[k]()

            def prepare():
                dve.wait_ge(weights_loaded, 16 * WEIGHTS)
                dve.tensor_scalar(restc, alphac, -1.0, 1.0, ALU.mult, ALU.add)
                st.mark(dve.tensor_scalar(dsub[:, :], dsub[:, :], 0.0, -1.0, ALU.is_gt, ALU.add))
                dve.wait_ge(qv_summed, 1)
                st.then(dve.tensor_copy(qv, one[:, 0:6]))
                for c, i in enumerate((1, 3, 0, 2)):
                    ins = dve.tensor_copy(proj1[:, D + c:D + c + 1], qv[:, i:i + 1])
                ins.then_inc(qv_placed, 1)
            masks(0, at([0, 1, 6, 8, 14, 16], own[1] + own[2] + own[3]))
            prepare()
            dve.wait_ge(consts_made, 1)

            def post0(q):
                def divisors():
                    dve.wait_ge(acc_taken, (q + 1) * NB)
                    st.then(dve.tensor_scalar(inv[:, :], Ud, alphac, restc, ALU.mult, ALU.add))
                    st.then(dve.tensor_scalar(zero[:, :], inv[:, :], 0.0, None, ALU.is_equal))
                    st.then(dve.tensor_tensor(inv[:, :], inv[:, :], zero[:, :], ALU.add))
                    st.then(dve.reciprocal(inv[:, :], inv[:, :]))
                    st.then(dve.tensor_scalar(zero[:, :], zero[:, :], -1.0, 1.0, ALU.mult, ALU.add))
                    st.then(dve.tensor_tensor(inv[:, :], inv[:, :], zero[:, :], ALU.mult))

                def own_part():
                    dve.wait_ge(f_turned, q + Q)
                    st.then(dve.tensor_scalar(V3, blocks(G[:, 0, :, :], q)[:, :, 0:D], restc, None, ALU.mult))
                    st.then(dve.scalar_tensor_tensor(Uf, Uf, alphac, V3, ALU.mult, ALU.add))

                def divide():
                    st.then(dve.tensor_tensor(Uf, Uf, wide(inv), ALU.mult))

                def bias():
                    st.then(dve.tensor_tensor(Uf, Uf, bias0_b.unsqueeze(1).broadcast_to([P, S, D]), ALU.add))

                def add():
                    dve.scalar_tensor_tensor(blocks(X, q), Uf, 0.0, blocks(X, q), ALU.max, ALU.add)\
                        .then_inc(post_done, 1)
                    dve.wait_ge(post_done, q + 1)

                def self_loops():
                    dve.wait_ge(mask_made, (q + 1) * T)
                    for s in range(S):
                        ins = dve.tensor_tensor(diagonal(q, s), diagonal(q, s), ident[:, :], ALU.max)
                    st.mark(ins)
                return [divisors, own_part, divide, bias, add, self_loops]

            def stage0(q):
                masks(q, at([1, 3, 5, 6, 7, 10, 8, 9, 14, 16], post0(q - 1) + feed(1, q - 1 + Q, q - 1)))
            quarters(dve, 1, Q - 1, stage0, st, 23)
            last = post0(Q - 1)
            for step in last[:-1] + feed(1, 2 * Q - 1, Q - 1) + last[-1:]:
                step()
            dve.wait_ge(f_placed, 2 * Q)
            top_of(1)
            top_of(2)
            scale_g(1, 0)

            def post1(h, q):
                j = q + h * Q
                n = j + Q

                def divide():
                    dve.wait_ge(acc_taken, (n + 1) * NB)
                    st.then(dve.reciprocal(inv[:, :], Ud))
                    st.mark(dve.tensor_tensor(Uf, Uf, wide(inv), ALU.mult))

                def residual():
                    dve.wait_ge(in_again, j + 1)
                    st.wait()
                    st.then(dve.tensor_tensor(Uf, Uf, V3, ALU.add))

                def stat():
                    statistics(lambda s: U3[:, s, 0:D], n_var)

                def scal():
                    if h == 0:
                        dve.wait_ge(f_norm, q + 2 * Q + 1)
                    else:
                        dve.wait_ge(f_norm, q + 3 * Q)
                    scales(n_dev, j + 1, n_scale)

                def elu():
                    dve.wait_ge(exp_made, j + 1)
                    ins = dve.scalar_tensor_tensor(V3, V3, 1.0, mixed3, ALU.min, ALU.add)
                    if h == 0:
                        ins.then_inc(post_done, 1)
                    else:
                        st.mark(ins)

                def both():
                    dve.wait_ge(back, 16 * (q + 1))
                    st.wait()
                    st.then(dve.scalar_tensor_tensor(V3, V3, 1.0 / HEADS, kept, ALU.mult, ALU.add))
                    dve.tensor_tensor(blocks(X, q), blocks(X, q), V3, ALU.add).then_inc(post_done, 1)
                    dve.wait_ge(post_done, n + 1)

                def own_pattern():
                    dve.wait_ge(e_made, (n - Q + 1) * T)
                    for s in range(S):
                        ins = dve.scalar_tensor_tensor(diagonal(q, s), ident[:, :], blocks(dsub, q, 1, s),
                                                       diagonal(q, s), ALU.mult, ALU.add)
                    st.mark(ins)
                steps = [divide, residual, stat, scal, elu]
                return steps if h == 0 else steps + [both, own_pattern]

            def scaling(h):
                return {3 + S * (i - 1): lambda i=i: scale_g(h, i) for i in range(1, Q)}

            run(1, 0, scaling(1))
            quarters(dve, 1, Q - 1, lambda q: run(1, q, at([3, 6, 7, 9, 18], post1(0, q - 1))), st, 7)
            dve.wait_ge(f_placed, 3 * Q)
            scale_g(2, 0)
            hooks = at([1, 6, 7, 9, 18], post1(0, Q - 1))
            hooks.update({k + 1: f for k, f in scaling(2).items()})
            run(2, 0, hooks)

            dve.wait_ge(w2_loaded, 16)
            dve.tensor_copy(proj2[:, D:D + 1], qv[:, 5:6])
            dve.tensor_copy(proj2[:, D + 1:D + 2], qv[:, 4:5]).then_inc(qv2_placed, 1)

            def stage2(q):
                run(2, q, at([3, 6, 7, 9, 18, 19, 13, 20, 22, 28], post1(1, q - 1) + feed(3, q - 1 + 3 * Q, q - 1)))
            quarters(dve, 1, Q - 2, stage2, st, 14)
            stage2(Q - 1)
            last = post1(1, Q - 1)
            for step in last[:-1] + feed(3, 4 * Q - 1, Q - 1) + last[-1:]:
                step()
            dve.wait_ge(half_summed, Q)
            dve.tensor_scalar(hmean, hmean, 1.0 / N, None, ALU.mult).then_inc(mean_ready, 1)
            dve.wait_ge(f_placed, 4 * Q)
            dve.wait_ge(mean_spread, 1)
            dve.tensor_copy(mean2, mixed[:, 0:D]).then_inc(mean_kept, 1)
            top_of(3)
            scale_g(3, 0)

            def post2(q):
                def divisors():
                    dve.wait_ge(acc_taken, (q + 3 * Q + 1) * NB)
                    st.then(dve.tensor_scalar(zero[:, :], Ud, 0.0, None, ALU.is_equal))
                    st.then(dve.tensor_tensor(inv[:, :], Ud, zero[:, :], ALU.add))
                    st.then(dve.reciprocal(inv[:, :], inv[:, :]))

                def divide():
                    st.mark(dve.tensor_tensor(Uf, Uf, wide(inv), ALU.mult))

                def lonely():
                    st.then(dve.tensor_tensor(V3, mean2.unsqueeze(1).broadcast_to([P, S, D]), wide(zero), ALU.mult))
                    st.then(dve.tensor_tensor(Uf, Uf, V3, ALU.add))

                def add():
                    dve.scalar_tensor_tensor(blocks(X, q), Uf, 0.0, blocks(X, q), ALU.max, ALU.add)\
                        .then_inc(post_done, 1)
                    dve.wait_ge(post_done, q + 3 * Q + 1)
                return [divisors, divide, lonely, add]

            dve.wait_ge(mean_kept, 1)
            hooks = scaling(3)
            hooks[27] = lambda: st.mark(dve.memset(G[:, 0, :, D], 1.0))
            run(3, 0, hooks)

            def stage3(q):
                run(3, q, at([3, 4, 6, 8, 11, 13], post2(q - 1) + feed(4, q - 1 + 4 * Q, q - 1)))
            quarters(dve, 1, Q - 2, stage3, st, 10)
            stage3(Q - 1)
            for step in post2(Q - 1) + feed(4, 5 * Q - 1, Q - 1):
                step()

            def post3(q):
                dve.wait_ge(acc_taken, (q + 4 * Q + 1) * NB)
                st.then(dve.tensor_scalar(zero[:, :], Ud, 0.0, None, ALU.is_equal))
                st.then(dve.tensor_tensor(inv[:, :], Ud, zero[:, :], ALU.add))
                st.then(dve.reciprocal(inv[:, :], inv[:, :]))
                st.then(dve.tensor_scalar(zero[:, :], zero[:, :], -1.0, 1.0, ALU.mult, ALU.add))
                st.then(dve.tensor_tensor(inv[:, :], inv[:, :], zero[:, :], ALU.mult))
                st.then(dve.tensor_tensor(Uf, Uf, wide(inv), ALU.mult))
                if not fixed(q):
                    dve.wait_ge(stored, q * 16)
                dve.tensor_tensor(V3, Uf, blocks(X, q), ALU.add).then_inc(post_done, 1)
            post3(0)
            quarters(dve, 1, Q - 1, post3, st, 6)


def kernel(**inputs):
    import numpy as np
    import concourse.bacc as bacc
    from concourse.bass_utils import run_bass_kernel_spmd

    nc = bacc.Bacc("TRN2", target_bir_lowering=False, num_devices=1)
    g = {k: np.asarray(v) for k, v in inputs.items()}
    given = {
        "x": g["x"], "adj": g["adj"], "adj_t": g["adj"].T, "diag": g["adj"].diagonal().reshape(-1, P).T,
        "alpha": g["L0_gnn_alpha"],
        "w0_t": g["L0_gnn_W"].T, "bias0": g["L0_gnn_b"],
        "ff0": g["L1_gnn_ff0_w"], "ff0_t": g["L1_gnn_ff0_w"].transpose(0, 2, 1),
        "ff1_t": g["L1_gnn_ff1_w"].transpose(0, 2, 1), "attn": g["L1_gnn_attn_w"].reshape(4, P).T,
        "g1": g["L1_gnn_g1"], "b1": g["L1_gnn_b1"], "g2": g["L1_gnn_g2"], "b2": g["L1_gnn_b2"],
        "w2": g["L2_gnn_W"], "w2_t": g["L2_gnn_W"].T, "a2": g["L2_gnn_a"].reshape(2, P).T,
    }
    arrays, args = {}, []
    for name, a in given.items():
        a = np.ascontiguousarray(a)
        arrays[f"in_{name}"] = a
        args.append(nc.dram_tensor(f"in_{name}", a.shape, mybir.dt.from_np(a.dtype), kind="ExternalInput").ap())
    args.append(nc.dram_tensor("out_x", g["x"].shape, F32, kind="ExternalOutput").ap())
    args.append(nc.dram_tensor("kept0", (P, g["x"].size // P), F32, kind="Internal").ap())
    graph_layers(nc, *args)
    r = run_bass_kernel_spmd(nc, [arrays], core_ids=[0])
    return r.results[0]["out_x"]
```

```python
from contextlib import ExitStack

import concourse.bass as bass
from concourse import mybir

P = 128
ALU = mybir.AluOpType
ACT = mybir.ActivationFunctionType
F32 = mybir.dt.float32
U8 = mybir.dt.uint8
AX_X = mybir.AxisListType.X
EPS = 1e-5


class Steps:

    def __init__(self, eng, sem):
        self.eng, self.sem, self.done, self.extra = eng, sem, 0, None

    def mark(self, ins):
        ins.then_inc(self.sem, 1)
        self.done += 1

    def wait(self):
        self.eng.wait_ge(self.sem, self.done if self.extra is None else self.extra + self.done)

    def then(self, ins):
        self.mark(ins)
        self.wait()

    def enter(self, turn, per_turn):
        self.start, self.per_turn, self.extra = self.done, per_turn, turn * per_turn

    def leave(self, turns):
        assert self.done - self.start == self.per_turn, (self.done - self.start, self.per_turn)
        self.done, self.extra = self.start + self.per_turn * turns, None


def graph_layers(nc, x, adj, adj_t, diag, alpha, w0_t, bias0, ff0, ff0_t, ff1_t, attn, g1, b1, g2, b2,
                 w2, w2_t, a2, out, inputs1):
    N, D = x.shape
    T = N // P
    Q = 4
    S = T // Q
    QC = S * P
    DW = D + 1
    PW = D + 4
    HEADS = 2
    BANK = 512
    NB = (S + 2) // 3
    STREAM = 4
    DEEP = 8
    EB = 3
    WEIGHTS = 15
    WARM = 38

    with ExitStack() as ctx:
        def sb(name, shape, dt=F32):
            return ctx.enter_context(nc.sbuf_tensor(name, shape, dt))

        def sem(name):
            return ctx.enter_context(nc.semaphore(name))

        mask = sb("mask", [P, T * N], U8)
        X = sb("X", [P, T, D])
        G = sb("G", [P, 2, T, DW])
        ring = sb("ring", [P, 5, QC])
        U = sb("U", [P, S * DW])
        V = sb("V", [P, S, D])
        ident = sb("ident", [P, P])
        ff1T = sb("ff1T", [P, HEADS, D])
        score1 = sb("score1", [P, T, 4])
        score2 = sb("score2", [P, T, 2])
        norms = sb("norms", [P, 4, T])
        stats = sb("stats", [P, S, 6])
        mean = sb("mean", [P, S])
        parts = sb("parts", [P, 3, S])
        var = sb("var", [P, S])
        dev = sb("dev", [P, S])
        scale = sb("scale", [P, S])
        shift = sb("shift", [P, S])
        cols = sb("cols", [P, 32])
        rq = sb("rq", [P, S])
        inv = sb("inv", [P, S])
        zero = sb("zero", [P, S])
        dsub = sb("dsub", [P, T])

        R = ring[:, 0, :]
        E = [ring[:, 1 + i, :] for i in range(EB)]
        spare = ring[:, 4, :]
        w0T = spare[:, 0:D]
        bias0_b = spare[:, D:2 * D]
        proj1 = spare[:, 2 * D:2 * D + PW]
        o = 2 * D + PW
        ff0T1 = spare[:, o:o + D]
        ff0raw = [spare[:, o + (1 + h) * D:o + (2 + h) * D] for h in range(HEADS)]
        w2raw = spare[:, o + 3 * D:o + 4 * D]
        proj2 = spare[:, o + D:o + 2 * D + 2]
        mean2 = spare[:, o + 2 * D + 2:o + 3 * D + 2]
        fold, later = [spare[:, o + 4 * D + i * S:o + 4 * D + (i + 1) * S] for i in range(2)]
        stream3 = mask[:, 0:DEEP * QC * 4].bitcast(F32).rearrange("p (s c) -> p s c", c=QC)
        U3 = U[:, :].rearrange("p (s d) -> p s d", d=DW)
        g1c, b1c, g2c, b2c, alphac, restc, top, bigc, wbias, vbias = [cols[:, i:i + 1] for i in range(10)]
        twice, apart, squares = [parts[:, i, :] for i in range(3)]
        attnc = cols[:, 10:16]
        qv = cols[:, 16:22]
        hpart = [cols[:, 22 + c:23 + c] for c in range(2)]
        hmean = cols[:, 24:25]
        seen = cols[:, 25:26]
        first_top, fall, vfix, wfix = [cols[:, i:i + 1] for i in range(26, 30)]
        warm = {ACT.Sqrt: cols[:, 30:31], ACT.Exp: cols[:, 31:32]}

        acc = ctx.enter_context(nc.psum_tensor("acc", [P, NB, BANK], F32))
        turn = ctx.enter_context(nc.psum_tensor("turn", [P, 2 * BANK], F32))
        mix = ctx.enter_context(nc.psum_tensor("mix", [P, NB, BANK], F32))
        mixed = mix[:, 0:2, :].rearrange("p b c -> p (b c)")
        mixed3 = mixed.rearrange("p (s d) -> p s d", d=D)
        one = mix[:, 2, 0:P]

        SLOPE = {1: 0.01, 2: 0.01, 3: 0.2}
        rank = {1: score1[:, :, 0], 2: score1[:, :, 1], 3: score2[:, :, 0]}
        row = {1: score1[:, :, 2], 2: score1[:, :, 3], 3: score2[:, :, 1]}

        EARLY = T - S
        early_top = {1: 1, 3: 4}
        late_top = {1: 2, 2: 3, 3: 5}
        kept_rows = {1: 2, 2: 6, 3: 11}
        fixes = {1: 1, 3: 2}

        x_first, rest_normal = sem("x_first"), sem("rest_normal")
        x_loaded = [sem(f"x_loaded{q}") for q in range(Q)]
        w0_loaded, weights_loaded, w2_loaded = sem("w0_loaded"), sem("weights_loaded"), sem("w2_loaded")
        saved, back, stored = sem("saved"), sem("back"), sem("stored")
        last_made = sem("last_made")
        slot_loaded = [sem(f"slot_loaded{i}") for i in range(STREAM)]
        deep_loaded = [sem(f"deep_loaded{i}") for i in range(DEEP)]
        consts_made, ident_zero, dve_step = sem("consts_made"), sem("ident_zero"), sem("dve_step")
        qv_summed, qv_placed, qv2_placed = sem("qv_summed"), sem("qv_placed"), sem("qv2_placed")
        f_var, f_dev, f_scale, f_norm = sem("f_var"), sem("f_dev"), sem("f_scale"), sem("f_norm")
        f2_var, f2_dev, f2_scale, f2_in = sem("f2_var"), sem("f2_dev"), sem("f2_scale"), sem("f2_in")
        f_turned, f_wide, f_projected, f_placed = sem("f_turned"), sem("f_wide"), sem("f_projected"), sem("f_placed")
        top_placed, top_spread, bias_made, row_shifted = sem("top_placed"), sem("top_spread"), sem("bias_made"), sem("row_shifted")
        rq_shifted, fix_made = sem("rq_shifted"), sem("fix_made")
        v_made, w_made, r_made = sem("v_made"), sem("w_made"), sem("r_made")
        g_scaled = [sem(f"g_scaled{part}") for part in range(Q)]
        half_summed, mean_ready, mean_spread, mean_kept = sem("half_summed"), sem("mean_ready"), sem("mean_spread"), sem("mean_kept")
        fall_made, fold_made, fixed_v, fixed_w = sem("fall_made"), sem("fold_made"), sem("fixed_v"), sem("fixed_w")
        acc_paused = [sem(f"acc_paused{b}") for b in range(NB - 1)]
        acc_scaled = sem("acc_scaled")
        rq_ready, rows_spread, rows_kept = sem("rq_ready"), sem("rows_spread"), sem("rows_kept")
        mask_made, slot_used, e_made, e_used, deep_used = sem("mask_made"), sem("slot_used"), sem("e_made"), sem("e_used"), sem("deep_used")
        acc_summed = [sem(f"acc_summed{b}") for b in range(NB)]
        acc_taken = sem("acc_taken")
        own_made = sem("own_made")
        inv_ready, divided = sem("inv_ready"), sem("divided")
        post_done = sem("post_done")
        n_var, n_dev, n_scale, n_norm = sem("n_var"), sem("n_dev"), sem("n_scale"), sem("n_norm")
        n_turned, n_wide, ff_done, exp_made, half_made = sem("n_turned"), sem("n_wide"), sem("ff_done"), sem("exp_made"), sem("half_made")
        elu_made, input_made = sem("elu_made"), sem("input_made")

        block = ctx.enter_context(nc.Block())

        def fixed(v):
            return isinstance(v, int)

        def span(t, start, n):
            return t[:, start:start + n] if fixed(start) else t[:, bass.ds(start, n)]

        def blocks(t, q, n=S, at=0):
            return span(t, q * S + at, n)

        def width(b):
            return min(3, S - 3 * b)

        def quarters(eng, first, last, body, steps=None, per_turn=0):
            with eng.Fori(first, last + 1) as q:
                if steps:
                    steps.enter(q - first if first else q, per_turn)
                body(q)
            if steps:
                steps.leave(last + 1 - first)

        def wait(eng, signal, count):
            if not fixed(count) or count > 0:
                eng.wait_ge(signal, count)

        @block.sync
        def _(sp):
            def load_x(t, n, loaded):
                sp.dma_start(X[:, t:t + n, :], x[t * P:(t + n) * P, :].rearrange("(s p) d -> p s d", p=P)).then_inc(loaded, 16)

            def stream(src, slots, loaded, used, h, q, some=range(T)):
                L = len(loaded)
                for k in some:
                    if k >= L:
                        sp.wait_ge(used, q * (T - 1) + k - L + 1)
                    elif not fixed(q) and k == L - 1:
                        sp.wait_ge(acc_summed[NB - 1], q + h * Q)
                    elif not fixed(q):
                        sp.wait_ge(used, q * (T - 1) + k - L + 2)
                    sp.dma_start(slots(k % L), span(src[k * P:(k + 1) * P, :], q * QC, QC))\
                        .then_inc(loaded[k % L], 16)

            def layer0(q, some=range(T)):
                stream(adj_t, lambda s: ring[:, s, :], slot_loaded, slot_used, 0, q, some)

            def layer3(q):
                stream(adj, lambda s: stream3[:, s, :], deep_loaded, deep_used, 4, q)

            load_x(0, S // 2, x_first)
            load_x(S // 2, S // 2, x_loaded[0])
            sp.dma_start(w0T, w0_t).then_inc(w0_loaded, 16)
            layer0(0, range(2))
            load_x(S, S, x_loaded[1])
            layer0(0, range(2, STREAM))
            load_x(2 * S, S, x_loaded[2])
            load_x(3 * S, S, x_loaded[3])
            loads = [(bias0_b, bias0.partition_broadcast(P)), (alphac, alpha.partition_broadcast(P)),
                     (w2raw, w2_t), (attnc[:, 0:4], attn), (attnc[:, 4:6], a2), (dsub[:, :], diag),
                     (proj1[:, 0:D], ff0_t[0]), (ff0T1, ff0_t[1])]
            loads += [(ff0raw[h], ff0[h]) for h in range(HEADS)]
            loads += [(c, v.rearrange("(c o) -> c o", o=1)) for c, v in ((g1c, g1), (b1c, b1), (g2c, g2), (b2c, b2))]
            loads += [(ff1T[:, :, :], ff1_t.rearrange("h c o -> c h o"))]
            assert len(loads) == WEIGHTS
            for dst, src in loads:
                sp.dma_start(dst, src).then_inc(weights_loaded, 16)
            layer0(0, range(STREAM, T))
            quarters(sp, 1, Q - 1, layer0)

            sp.wait_ge(qv_summed, 1)
            sp.dma_start(proj2[:, 0:D], w2).then_inc(w2_loaded, 16)

            sp.wait_ge(saved, 16 * Q)

            def bring_back(q):
                if fixed(q):
                    sp.wait_ge(post_done, 2 * Q)
                else:
                    sp.wait_ge(f_turned, q + 3 * Q)
                sp.dma_start(V[:, :, :].rearrange("p s d -> p (s d)"), span(inputs1, q * QC, QC)).then_inc(back, 16)
            bring_back(0)
            quarters(sp, 1, Q - 1, bring_back)

            sp.wait_ge(e_made, 3 * Q * T)
            layer3(0)
            quarters(sp, 1, Q - 1, layer3)
            for b in range(NB):
                sp.wait_ge(last_made, b + 1)
                some = slice(3 * b, 3 * b + width(b))
                sp.dma_start(out.rearrange("(t p) d -> p t d", p=P)[:, (Q - 1) * S:, :][:, some, :], V[:, some, :])\
                    .then_inc(stored, 16)
            sp.wait_ge(stored, 16 * (Q - 1 + NB))

        @block.gpsimd
        def _(pool):
            nc.gpsimd.memset(ident[:, :], 0.0).then_inc(ident_zero, 1)
            pool.wait_ge(ident_zero, 1)
            nc.gpsimd.affine_select(out=ident[:, :], in_=ident[:, :], compare_op=ALU.not_equal, fill=1.0,
                                    base=0, pattern=[[-1, P]], channel_multiplier=1).then_inc(consts_made, 1)

        @block.tensor
        def _(pe):
            def products(n, k, lhs, g, done, fix):
                for s in range(S):
                    b = s // 3
                    if fix and k == EARLY and s % 3 == 0:
                        pe.wait_ge(acc_scaled, fix * NB - NB + b + 1)
                    if k == 0 and s % 3 == 0:
                        wait(pe, acc_taken, 0 if fixed(n) and n == 0 else n * NB - NB + b + 1)
                    mm = pe.matmul(acc[:, b, (s % 3) * DW:(s % 3) * DW + DW], lhs[:, s * P:(s + 1) * P], g,
                                   start=(k == 0 and s % 3 == 0), stop=(k == T - 1), skip_group_check=True)
                    if k == T - 1 and (s % 3 == 2 or s == S - 1):
                        mm.then_inc(acc_summed[b], 1)
                    elif s == S - 1:
                        mm.then_inc(done, 1)
                    elif fix and k == EARLY - 1 and s % 3 == 2:
                        mm.then_inc(acc_paused[b], 1)

            def spread(col, dst):
                return pe.transpose(dst, col.broadcast_to([P, P]), ident[:, :])

            def turn_v():
                for s in range(S):
                    mm = pe.transpose(turn[:, s * P:(s + 1) * P], V[:, s, :], ident[:, :])
                return mm

            def feed(p, weights, wide, spreads, posts):
                def turned():
                    pe.wait_ge(f_norm, p + 1)
                    if fixed(p) and p == 0:
                        pe.wait_ge(rest_normal, 1)
                    wait(pe, rows_kept, spreads)
                    turn_v().then_inc(f_turned, 1)

                def project():
                    pe.wait_ge(f_wide, p + 1)
                    if fixed(p) and p == 2 * Q:
                        pe.wait_ge(bias_made, late_top[2])
                    wait(pe, f_placed, p)
                    wait(pe, post_done, posts)
                    for s in range(S):
                        mm = pe.matmul(mix[:, s // 3, (s % 3) * PW:(s % 3) * PW + wide],
                                       U[:, s * P:(s + 1) * P], weights, start=True, stop=True,
                                       skip_group_check=True)
                    mm.then_inc(f_projected, 1)
                return turned, project

            def post1(j, spreads, feeds):
                def turned():
                    pe.wait_ge(n_norm, j + 1)
                    pe.wait_ge(rows_kept, spreads)
                    turn_v().then_inc(n_turned, 1)

                def apply(h):
                    pe.wait_ge(n_wide, j + 1)
                    pe.wait_ge(f_placed, feeds)
                    for s in range(S):
                        mm = pe.matmul(mixed[:, s * P:(s + 1) * P], U[:, s * P:(s + 1) * P], ff1T[:, h, :],
                                       start=True, stop=True, skip_group_check=True)
                    mm.then_inc(ff_done, 1)
                return turned, apply

            def spread_top(i):
                pe.wait_ge(top_placed, i)
                spread(top, one).then_inc(top_spread, 1)

            def spread_rows(m, feeds=0):
                wait(pe, f_wide, feeds)
                pe.wait_ge(rq_ready, m + 1)
                wait(pe, rows_kept, m)
                for s in range(S):
                    mm = spread(rq[:, s:s + 1], turn[:, s * P:(s + 1) * P])
                mm.then_inc(rows_spread, 1)

            def run(h, q, hooks):
                n = q + h * Q
                for k in range(T):
                    if h == 0:
                        pe.wait_ge(slot_loaded[k % STREAM], (q * (T // STREAM) + k // STREAM + 1) * 16)
                        pe.wait_ge(mask_made, q * T + k + 1)
                        if fixed(q) and q == 0 and k % S == 0:
                            pe.wait_ge(f_placed, k // S + 1)
                        lhs, used = ring[:, k % STREAM, :], slot_used
                    elif h == 4:
                        pe.wait_ge(deep_loaded[k % DEEP], (q * (T // DEEP) + k // DEEP + 1) * 16)
                        if fixed(q) and q == 0 and k % S == 0:
                            pe.wait_ge(f_norm, 4 * Q + k // S + 1)
                        lhs, used = stream3[:, k % DEEP, :], deep_used
                    else:
                        pe.wait_ge(e_made, (n - Q) * T + k + 1)
                        if fixed(q) and q == 0 and k % S == 0:
                            if h == 2:
                                pe.wait_ge(f_placed, 2 * Q + k // S + 1)
                            else:
                                pe.wait_ge(g_scaled[k // S], fixes[h])
                        lhs, used = E[k % EB], e_used
                        if k == 0 and h != 2 and not (fixed(q) and q == 0):
                            pe.wait_ge(fixed_v, fixes[h])
                    products(n, k, lhs, G[:, h % 2, k, :], used, fixes[h] if h in fixes and fixed(q) and q == 0 else 0)
                    if k in hooks:
                        hooks[k]()

            pe.wait_ge(consts_made, 1)
            for i in range(WARM):
                pe.transpose(one, ident[:, :], ident[:, :])
            pe.wait_ge(w0_loaded, 16)
            own = [feed(p, w0T, D, 0, 0) for p in range(Q)]
            own[0][0]()
            own[0][1]()

            def scores_behind_projections():
                pe.wait_ge(weights_loaded, 16 * WEIGHTS)
                pe.wait_ge(f_placed, Q)
                for h, raw in enumerate(ff0raw + [w2raw]):
                    mm = pe.matmul(one[:, 2 * h:2 * h + 2], raw, attnc[:, 2 * h:2 * h + 2], start=True, stop=True,
                                   skip_group_check=True)
                mm.then_inc(qv_summed, 1)
            run(0, 0, {2: own[1][0], 4: own[1][1], 10: own[2][0], 13: own[2][1], 18: own[3][0], 21: own[3][1],
                       28: scores_behind_projections})

            def stage0(q, more={}):
                turned, project = feed(Q + q - 1, proj1, PW, 0, q)
                run(0, q, {19: turned, 22: project} | more)
            pe.wait_ge(qv_placed, 1)
            quarters(pe, 1, Q - 2, stage0)
            stage0(Q - 1, {25: lambda: spread_top(early_top[1]), 28: lambda: spread_rows(0)})

            def stage1(q):
                m = q + kept_rows[1]
                first = fixed(q) and q == 0
                turned, project = feed(q + 2 * Q, ff0T1, D, m, q + Q)
                if first:
                    own = feed(2 * Q - 1, proj1, PW, 1, Q)
                    hooks = {17: own[0], 18: own[1], 19: lambda: spread_top(late_top[1]), 21: lambda: spread_rows(1),
                             25: lambda: spread_top(late_top[2]), 26: turned, 28: lambda: spread_rows(m, 2 * Q + 1), 29: project}
                else:
                    rows_turned, apply = post1(q - 1, m, q + 2 * Q)
                    hooks = {12: rows_turned, 14: lambda: apply(0), 23: turned, 26: project, 27: lambda: spread_rows(m, q + 2 * Q + 1)}
                run(1, q, hooks)
            stage1(0)
            quarters(pe, 1, Q - 1, stage1)

            def stage2(q):
                m = q + kept_rows[2]
                first = fixed(q) and q == 0
                rows_turned, apply = post1(q - 1 + Q, m, 3 * Q if first else q - 1 + 3 * Q)
                hooks = {11: rows_turned, 13 if first else 12: lambda: apply(0 if first else 1)}
                if not first:
                    turned, project = feed(q - 1 + 3 * Q, proj2, D + 2, m, q + 2 * Q)
                    hooks.update({25: turned, 26 if fixed(q) else 29: project})
                if fixed(q) and q == Q - 1:
                    hooks[27] = lambda: spread_top(early_top[3])
                    hooks[29] = lambda: spread_rows(m)
                else:
                    hooks[27] = lambda: spread_rows(m, 0 if first else q + 3 * Q)
                run(2, q, hooks)
            stage2(0)
            pe.wait_ge(qv2_placed, 1)
            quarters(pe, 1, Q - 2, stage2)
            stage2(Q - 1)

            def spread_mean():
                pe.wait_ge(mean_ready, 1)
                pe.wait_ge(f_placed, 4 * Q)
                pe.matmul(mixed[:, 0:D], hmean.broadcast_to([P, P]), proj2[:, 0:D], start=True, stop=True)\
                    .then_inc(mean_spread, 1)
            rows_turned, apply = post1(2 * Q - 1, kept_rows[3] - 1, 4 * Q - 1)
            turned, project = feed(4 * Q - 1, proj2, D + 2, kept_rows[3] - 1, 3 * Q)
            run(3, 0, {8: rows_turned, 9: lambda: apply(1), 18: turned, 19: project,
                       20: lambda: spread_top(late_top[3]), 21: lambda: spread_rows(kept_rows[3] - 1), 26: spread_mean,
                       28: lambda: spread_rows(kept_rows[3])})

            def stage3(q):
                run(3, q, {28: lambda: spread_rows(q + kept_rows[3])})
            quarters(pe, 1, Q - 2, stage3)
            run(3, Q - 1, {})

            run(4, 0, {})
            quarters(pe, 1, Q - 1, lambda q: run(4, q, {}))

        @block.scalar
        def _(act):
            def settle():
                act.copy(seen, ident[:, 0:1])

            def ready(func):
                act.activation(warm[func], ident[:, 0:1], func)

            def normalise(dst, src, mul, add, func, done, n=S):
                for s in range(n):
                    ins = act.activation(dst(s), src(s), func, bias=add(s), scale=mul(s))
                if done is not None:
                    ins.then_inc(done, 1)

            def local(t):
                return lambda s: t[:, s:s + 1]

            def of_v(s):
                return V[:, s, :]

            def deviation(got, n, done):
                act.wait_ge(got, n)
                act.activation(dev[:, :], var[:, :], ACT.Sqrt).then_inc(done, 1)

            def widen(got, n, done, scale_=None, bias_=None, halves=None):
                act.wait_ge(got, n)
                for c in range(2):
                    src, dst = turn[:, c * BANK:(c + 1) * BANK], U[:, c * BANK:(c + 1) * BANK]
                    if halves is not None:
                        ins = act.activation(dst, src, ACT.Identity, accum_out=hpart[c])
                    elif scale_ is not None:
                        ins = act.activation(dst, src, ACT.Identity, bias=bias_, scale=scale_)
                    else:
                        ins = act.copy(dst, src)
                ins.then_inc(done, 1)

            def feed(h, p, q, between=(), ahead=None):
                def of_x(s):
                    return blocks(X, q, 1, s)[:, 0, :]
                if h == 2:
                    act.wait_ge(rows_kept, 1)
                    def known(i):
                        return lambda s: blocks(norms[:, i, :], q, 1, s)
                    settle()
                    normalise(of_v, of_x, known(0), known(1), ACT.Relu, f2_in)
                    act.wait_ge(f2_in, q + Q + 1)
                    normalise(of_v, of_v, known(2), known(3), ACT.Identity, f_norm)
                else:
                    deviation(f_var, p - Q + 1 if h > 2 else p + 1, f_dev)
                    act.wait_ge(f_scale, p - Q + 1 if h > 2 else p + 1)
                    settle()
                    if h == 4:
                        normalise(lambda s: blocks(G[:, 0, :, :], q, 1, s)[:, 0, 0:D], of_x, local(scale), local(shift),
                                  ACT.Relu, f_norm)
                        return
                    normalise(of_v, of_x, local(scale), local(shift), ACT.Relu, f2_in if h == 1 else f_norm,
                              S // 2 if fixed(p) and p == 0 else S)
                    if h == 1:
                        deviation(f2_var, q + 1, f2_dev)
                        act.wait_ge(f2_scale, q + 1)
                        normalise(of_v, of_v, local(scale), local(shift), ACT.Identity, f_norm)
                if ahead is not None:
                    ahead()
                if h in (1, 2):
                    widen(f_turned, p + 1, f_wide, g1c, b1c)
                elif h == 3:
                    wait(act, half_summed, 0 if fixed(q) and q == 0 else q * 1)
                    widen(f_turned, p + 1, f_wide, halves=True)
                else:
                    widen(f_turned, p + 1, f_wide)
                for step in between:
                    step()
                act.wait_ge(f_projected, p + 1)
                if h == 2:
                    act.wait_ge(v_made, late_top[2])
                    settle()
                    normalise(lambda s: blocks(G[:, 0, :, :], q, 1, s)[:, 0, 0:D],
                              lambda s: mix[:, s // 3, (s % 3) * PW:(s % 3) * PW + D],
                              lambda s: blocks(G[:, 0, :, :], q, 1, s)[:, 0, D:D + 1], lambda s: 0.0, ACT.Copy, f_placed)
                    return
                for b in range(NB):
                    c = width(b)
                    got = mix[:, b, 0:c * PW].rearrange("p (s d) -> p s d", d=PW)
                    ins = act.copy(blocks(G[:, h % 2, :, :], q, c, 3 * b)[:, :, 0:D], got[:, :, 0:D])
                    if h == 1:
                        ins = act.copy(blocks(score1, q, c, 3 * b), got[:, :, D:D + 4])
                    if h == 3:
                        ins = act.copy(blocks(score2, q, c, 3 * b), got[:, :, D:D + 2])
                ins.then_inc(f_placed, 1)

            def early_exponentials(h):
                s_ = SLOPE[h]
                act.wait_ge(bias_made, early_top[h])
                act.activation(G[:, h % 2, 0:EARLY, D], rank[h][:, 0:EARLY], ACT.Exp, bias=vbias, scale=s_).then_inc(v_made, 1)
                act.activation(rank[h][:, 0:EARLY], rank[h][:, 0:EARLY], ACT.Exp, bias=wbias, scale=1.0 - s_).then_inc(w_made, 1)
                act.wait_ge(rq_shifted, fixes[h])
                act.activation(rq[:, :], rq[:, :], ACT.Exp, scale=-(1.0 - s_)).then_inc(rq_ready, 1)

            def exponentials(h):
                s_ = SLOPE[h]
                lo = EARLY if h in fixes else 0
                act.wait_ge(bias_made, late_top[h])
                act.activation(G[:, h % 2, lo:T, D], rank[h][:, lo:T], ACT.Exp, bias=vbias, scale=s_).then_inc(v_made, 1)
                act.activation(rank[h][:, lo:T], rank[h][:, lo:T], ACT.Exp, bias=wbias, scale=1.0 - s_).then_inc(w_made, 1)
                act.wait_ge(row_shifted, h)
                act.activation(row[h], row[h], ACT.Exp, scale=-(1.0 - s_)).then_inc(r_made, 1)

            def late_rows(h):
                s_ = SLOPE[h]
                exponentials(h)
                act.wait_ge(fall_made, fixes[h])
                act.activation(fold, fold, ACT.Exp).then_inc(fold_made, 1)
                rows_columns(kept_rows[h] - 1, h, 0)
                act.activation(vfix, fall, ACT.Exp, scale=s_)
                act.activation(wfix, fall, ACT.Exp, scale=1.0 - s_).then_inc(fix_made, 1)
                act.wait_ge(rows_spread, kept_rows[h])
                act.wait_ge(e_made, (h - 1) * Q * T + EARLY)
                rows_out()

            def scale_g(h, part):
                act.wait_ge(v_made, early_top[h])
                for j in range(part * S, (part + 1) * S):
                    g = G[:, h % 2, j, :]
                    ins = act.activation(g[:, 0:D], g[:, 0:D], ACT.Copy, scale=g[:, D:D + 1])
                ins.then_inc(g_scaled[part], 1)

            def put_right(h):
                act.wait_ge(fix_made, fixes[h])
                act.activation(rank[h][:, 0:EARLY], rank[h][:, 0:EARLY], ACT.Copy, scale=wfix).then_inc(fixed_w, 1)
                act.wait_ge(e_used, (h - 1) * Q * (T - 1) + EARLY)
                for c in range(Q - 1):
                    g = G[:, h % 2, c * S:(c + 1) * S, :]
                    ins = act.activation(g, g, ACT.Copy, scale=vfix)
                ins.then_inc(fixed_v, 1)

            def rows_columns(m, h, q):
                if fixed(q) and q == 0:
                    act.wait_ge(r_made, h)
                wait(act, rows_spread, m)
                act.copy(rq[:, :], blocks(row[h], q)).then_inc(rq_ready, 1)

            def rows_out():
                act.copy(R[:, 0:BANK], turn[:, 0:BANK])
                act.copy(R[:, BANK:2 * BANK], turn[:, BANK:2 * BANK]).then_inc(rows_kept, 1)

            def rows_copy(h, q):
                act.wait_ge(rows_spread, q + kept_rows[h])
                act.wait_ge(e_made, (q + (h - 1) * Q) * T)
                rows_out()

            def next_columns(h, q):
                rows_columns(q + kept_rows[h] - 1, h, q)

            def divide(i, lonely=None):
                act.wait_ge(inv_ready, i + 1)
                settle()
                if lonely is not None:
                    normalise(of_v, lambda s: lonely, local(zero), lambda s: 0.0, ACT.Copy, None)
                normalise(lambda s: U3[:, s, 0:D], lambda s: U3[:, s, 0:D], local(inv), lambda s: 0.0, ACT.Copy, divided)
                ready(ACT.Sqrt)

            def layer_input(q):
                settle()
                normalise(of_v, lambda s: blocks(X, q, 1, s)[:, 0, :],
                          lambda s: blocks(norms[:, 0, :], q, 1, s), lambda s: blocks(norms[:, 1, :], q, 1, s),
                          ACT.Relu, input_made)
                act.wait_ge(input_made, q + 1)
                act.dma_start(span(inputs1, q * QC, QC), V[:, :, :].rearrange("p s d -> p (s d)")).then_inc(saved, 16)

            def take(n):
                wait(act, post_done, n)
                for b in range(NB):
                    w = width(b) * DW
                    act.wait_ge(acc_summed[b], n + 1)
                    act.copy(U[:, b * 3 * DW:b * 3 * DW + w], acc[:, b, 0:w]).then_inc(acc_taken, 1)

            def post1(h, q, beside=()):
                j = q + h * Q
                take(j + Q)
                ready(ACT.Sqrt)
                for step in beside:
                    step()
                deviation(n_var, j + 1, n_dev)
                act.wait_ge(n_scale, j + 1)
                if h == 0:
                    act.wait_ge(saved, q * 16 + 16)
                    settle()
                normalise(of_v, lambda s: U3[:, s, 0:D], local(scale), local(shift), ACT.Identity, n_norm)
                act.wait_ge(n_norm, j + 1)
                widen(n_turned, j + 1, n_wide, g2c, b2c)
                ready(ACT.Exp)
                act.wait_ge(ff_done, j + 1)
                act.activation(V[:, :, :], mixed3, ACT.Exp)
                act.activation(mixed3, mixed3, ACT.Relu).then_inc(exp_made, 1)
                if h == 0:
                    act.wait_ge(elu_made, q + 1)
                    act.activation(V[:, :, :], V[:, :, :], ACT.Copy, bias=-1.0, scale=1.0 / HEADS).then_inc(half_made, 1)
                    act.wait_ge(post_done, j + Q + 1)
                else:
                    ready(ACT.Sqrt)

            act.wait_ge(consts_made, 1)
            ready(ACT.Sqrt)
            act.wait_ge(x_first, 16)
            for q in range(Q):
                act.wait_ge(x_loaded[q], 16)
                feed(0, q, q)

            def post0(q):
                act.wait_ge(f_turned, q + Q)
                settle()
                act.activation(V[:, :, :], blocks(G[:, 0, :, :], q)[:, :, 0:D], ACT.Copy, scale=restc).then_inc(own_made, 1)
                take(q)
                divide(q)

            def stage0(q):
                post0(q - 1)
                act.wait_ge(post_done, q)
                feed(1, q - 1 + Q, q - 1)
            act.wait_ge(weights_loaded, 16 * WEIGHTS)
            act.wait_ge(qv_placed, 1)
            quarters(act, 1, Q - 1, stage0)
            early_exponentials(1)
            act.wait_ge(rows_spread, 1)
            act.wait_ge(slot_used, (Q - 1) * (T - 1) + T - STREAM + 1)
            rows_out()

            post0(Q - 1)
            scale_g(1, 2)
            act.wait_ge(post_done, Q)
            feed(1, 2 * Q - 1, Q - 1, [lambda: ready(ACT.Exp)])
            late_rows(1)
            next_columns(1, 1)
            feed(2, 2 * Q, 0, [lambda: layer_input(0), lambda: rows_copy(1, 1)],
                 ahead=lambda: (put_right(1), exponentials(2)))

            def stage1(q, following):
                next_columns(*following)
                post1(0, q - 1)
                feed(2, q + 2 * Q, q, [lambda: layer_input(q), lambda: rows_copy(*following)])
            quarters(act, 1, Q - 2, lambda q: stage1(q, (1, q + 1)))
            stage1(Q - 1, (2, 0))

            next_columns(2, 1)
            post1(0, Q - 1)
            rows_copy(2, 1)

            def stage2(q, between, beside=()):
                post1(1, q - 1, beside)
                act.wait_ge(post_done, q + 2 * Q)
                feed(3, q - 1 + 3 * Q, q - 1, between)

            def stage2_rows(q):
                next_columns(2, q + 1)
                stage2(q, [lambda: rows_copy(2, q + 1)])
            quarters(act, 1, Q - 2, stage2_rows)
            stage2(Q - 1, [lambda: ready(ACT.Exp)])
            early_exponentials(3)
            act.wait_ge(rows_spread, kept_rows[3] - 1)
            act.wait_ge(e_made, 2 * Q * T)
            rows_out()

            stage2(Q, [lambda: ready(ACT.Exp)], [lambda: scale_g(3, 1), lambda: scale_g(3, 2)])
            late_rows(3)
            next_columns(3, 1)
            put_right(3)
            rows_copy(3, 1)

            def stage3(q, rows=True):
                n = q - 1 + 3 * Q
                if rows:
                    next_columns(3, q + 1)
                take(n)
                divide(q - 1 + Q, mean2)
                act.wait_ge(post_done, q + 3 * Q)
                feed(4, q - 1 + 4 * Q, q - 1)
                if rows:
                    rows_copy(3, q + 1)
            act.wait_ge(mean_kept, 1)
            quarters(act, 1, Q - 2, stage3)
            stage3(Q - 1, rows=False)
            stage3(Q, rows=False)

            def store(q):
                take(q + 4 * Q)
                act.wait_ge(post_done, q + 4 * Q + 1)
                act.dma_start(span(out.rearrange("(t p) d -> p t d", p=P), q * S, S), V[:, :, :]).then_inc(stored, 16)
            quarters(act, 0, Q - 2, store)
            take(5 * Q - 1)

        @block.vector
        def _(dve):
            st = Steps(dve, dve_step)
            STAGE0, STAGE1, STAGE2, STAGE3 = 20, 6, 12, 7
            V3 = V[:, :, :]
            Uf = U3[:, :, 0:D]
            Ud = U3[:, :, D]

            def wide(t):
                return t[:, :].unsqueeze(2).broadcast_to([P, S, D])

            def statistics(src, made):
                def half():
                    for s in range(S // 2):
                        dve.bn_stats(stats[:, s, :], src(s))

                def rest():
                    for s in range(S // 2, S):
                        ins = dve.bn_stats(stats[:, s, :], src(s))
                    st.then(ins)
                    dve.tensor_tensor(twice, stats[:, :, 1], stats[:, :, 4], ALU.add)
                    dve.tensor_tensor(apart, stats[:, :, 1], stats[:, :, 4], ALU.subtract)
                    st.then(dve.tensor_tensor(squares, stats[:, :, 2], stats[:, :, 5], ALU.add))
                    dve.tensor_scalar(mean[:, :], twice, 0.5, None, ALU.mult)
                    dve.tensor_tensor(apart, apart, apart, ALU.mult)
                    st.then(dve.tensor_scalar(squares, squares, 1.0 / D, EPS, ALU.mult, ALU.add))
                    dve.scalar_tensor_tensor(var[:, :], apart, 0.25, squares, ALU.mult, ALU.add).then_inc(made, 1)
                return [half, rest]

            def scales(got, n, done, keep=None):
                dve.wait_ge(got, n)
                st.then(dve.reciprocal(scale[:, :], dev[:, :]))
                if keep is not None:
                    i, q = keep
                    st.mark(dve.tensor_copy(blocks(norms[:, i, :], q), scale[:, :]))
                ins = dve.scalar_tensor_tensor(shift[:, :], mean[:, :], -1.0, scale[:, :], ALU.mult, ALU.mult)
                if keep is not None:
                    st.then(ins)
                    ins = dve.tensor_copy(blocks(norms[:, i + 1, :], q), shift[:, :])
                ins.then_inc(done, 1)

            def feed(h, p, q):
                c = p - Q + 1 if h > 2 else p + 1

                def first_scales():
                    wait(dve, f_norm, p)
                    scales(f_dev, c, f_scale, keep=(0, q) if h == 1 else None)

                def input_ready():
                    dve.wait_ge(f2_in, q + 1)

                def second_scales():
                    scales(f2_dev, q + 1, f2_scale, keep=(2, q))

                def halves():
                    dve.wait_ge(f_wide, p + 1)
                    wait(dve, half_summed, 0 if fixed(q) and q == 0 else q * 1)
                    dve.scalar_tensor_tensor(hmean, hpart[0], hpart[1], hmean, ALU.add, ALU.add).then_inc(half_summed, 1)
                steps = statistics(lambda s: blocks(X, q, 1, s)[:, 0, :], f_var) + [first_scales]
                if h == 1:
                    half, rest = statistics(of_v, f2_var)
                    steps += [lambda: (input_ready(), half()), rest, second_scales]
                if h == 3:
                    steps += [halves]
                return steps

            def of_v(s):
                return V[:, s, :]

            def early_of(h):
                def first():
                    dve.wait_ge(f_placed, (2 * Q if h == 1 else 4 * Q) - 1)
                    dve.reduce_max(top, rank[h][:, 0:EARLY], AX_X).then_inc(top_placed, 1)

                def second():
                    i = early_top[h]
                    dve.wait_ge(top_spread, i)
                    wait(dve, w_made, i - 1)
                    st.then(dve.reduce_max(first_top, one, AX_X))
                    biases(h, first_top)
                    wait(dve, rows_spread, kept_rows[h] - 2)
                    dve.tensor_scalar(rq[:, :], row[h][:, 0:S], first_top, 0.0, ALU.add, ALU.max).then_inc(rq_shifted, 1)
                return [first, second]

            def biases(h, largest):
                dve.tensor_scalar(vbias, largest, -SLOPE[h], None, ALU.mult)
                dve.tensor_scalar(wbias, largest, -(1.0 - SLOPE[h]), None, ALU.mult).then_inc(bias_made, 1)

            def top_of(h):
                late = h in fixes

                def first():
                    dve.wait_ge(f_placed, 2 * Q if h < 3 else 4 * Q)
                    dve.reduce_max(top, rank[h][:, EARLY if late else 0:T], AX_X).then_inc(top_placed, 1)

                def second():
                    i = late_top[h]
                    dve.wait_ge(top_spread, i)
                    dve.wait_ge(w_made, i - 1)
                    if late:
                        wait(dve, fold_made, fixes[h] - 1)
                    st.then(dve.reduce_max(bigc, one, AX_X))
                    if late:
                        st.then(dve.tensor_tensor(bigc, bigc, first_top, ALU.max))
                    biases(h, bigc)
                    if late:
                        a = row[h][:, 0:S]
                        dve.tensor_tensor(fall, first_top, bigc, ALU.subtract)
                        dve.tensor_scalar(fold, a, first_top, None, ALU.add)
                        st.then(dve.tensor_scalar(later, a, bigc, None, ALU.add))
                        dve.scalar_tensor_tensor(fold, fold, SLOPE[h], fold, ALU.mult, ALU.max)
                        st.then(dve.scalar_tensor_tensor(later, later, SLOPE[h], later, ALU.mult, ALU.max))
                        dve.tensor_tensor(fold, fold, later, ALU.subtract).then_inc(fall_made, 1)
                    dve.tensor_scalar(row[h], row[h], bigc, 0.0, ALU.add, ALU.max).then_inc(row_shifted, 1)
                return [first, second]

            def scale_sums(h):
                dve.wait_ge(fold_made, fixes[h])
                for b in range(NB):
                    if b < NB - 1:
                        dve.wait_ge(acc_paused[b], fixes[h])
                    else:
                        dve.wait_ge(e_used, (h - 1) * Q * (T - 1) + EARLY)
                    c = width(b)
                    sums = acc[:, b, 0:c * DW].rearrange("p (s d) -> p s d", d=DW)
                    f = fold[:, 3 * b:3 * b + c].unsqueeze(2).broadcast_to([P, c, DW])
                    dve.tensor_tensor(sums, sums, f, ALU.mult).then_inc(acc_scaled, 1)

            def scale_g(h, part):
                if part == 0:
                    dve.wait_ge(v_made, early_top[h])
                elif part == Q - 1:
                    dve.wait_ge(v_made, late_top[h])
                gp = G[:, h % 2, part * S:(part + 1) * S, :]
                v = gp[:, :, D:D + 1].broadcast_to([P, S, D])
                dve.tensor_tensor(gp[:, :, 0:D], gp[:, :, 0:D], v, ALU.mult).then_inc(g_scaled[part], 1)

            def run(h, q, hooks):
                m = q + (h - 1) * Q
                early = fixed(q) and q == 0 and h in fixes
                dve.wait_ge(rows_kept, q + kept_rows[h] - (1 if early else 0))
                if early:
                    dve.wait_ge(w_made, early_top[h])
                elif fixed(q) and q == 0:
                    dve.wait_ge(w_made, late_top[h])
                elif h in fixes:
                    dve.wait_ge(fixed_w, fixes[h])
                for k in range(T):
                    if early and k == EARLY:
                        dve.wait_ge(rows_kept, kept_rows[h])
                        dve.wait_ge(w_made, late_top[h])
                    if k >= EB:
                        dve.wait_ge(e_used, m * (T - 1) + k - EB + 1)
                    elif fixed(q) and m == 0:
                        if k < EB - 1:
                            dve.wait_ge(slot_used, Q * (T - 1) - 1 + k)
                        else:
                            dve.wait_ge(acc_summed[NB - 1], Q)
                    elif k == 0:
                        wait(dve, e_used, m * (T - 1))
                    elif k == 1:
                        dve.wait_ge(acc_summed[NB - 1], m + Q)
                    dve.scalar_tensor_tensor(E[k % EB], R, rank[h][:, k:k + 1], span(mask, q * QC + k * N, QC),
                                             ALU.max, ALU.mult).then_inc(e_made, 1)
                    if k in hooks:
                        hooks[k]()

            def diagonal(q, s):
                return span(mask, q * (S * (N + P)) + s * (N + P), P)

            def at(ks, steps):
                assert len(ks) == len(steps)
                return dict(zip(ks, steps))

            for i in range(2):
                dve.memset(G[:, i, :, D], 1.0)
            st.mark(dve.memset(hmean, 0.0))
            own = [feed(0, p, p) for p in range(Q)]
            dve.wait_ge(x_first, 16)
            own[0][0]()
            dve.wait_ge(x_loaded[0], 16)
            own[0][1]()
            own[0][2]()
            dve.wait_ge(f_scale, 1)
            for s in range(S // 2, S):
                ins = dve.tensor_scalar(V[:, s, :], X[:, s, :], scale[:, s:s + 1], shift[:, s:s + 1], ALU.mult, ALU.add)
            st.then(ins)
            dve.tensor_scalar(V[:, S // 2:, :], V[:, S // 2:, :], 0.0, None, ALU.max).then_inc(rest_normal, 1)

            def own_feed(q):
                return [lambda: (dve.wait_ge(x_loaded[q], 16), own[q][0]())] + own[q][1:]

            def masks(q, hooks):
                for k in range(T):
                    dve.wait_ge(slot_loaded[k % STREAM], (q * (T // STREAM) + k // STREAM + 1) * 16)
                    dve.tensor_scalar(span(mask, q * QC + k * N, QC), ring[:, k % STREAM, :], 0.0, None,
                                      ALU.is_gt).then_inc(mask_made, 1)
                    if k in hooks:
                        hooks[k]()

            def prepare():
                dve.wait_ge(weights_loaded, 16 * WEIGHTS)
                dve.tensor_scalar(restc, alphac, -1.0, 1.0, ALU.mult, ALU.add)
                st.mark(dve.tensor_scalar(dsub[:, :], dsub[:, :], 0.0, -1.0, ALU.is_gt, ALU.add))
                dve.wait_ge(qv_summed, 1)
                st.then(dve.tensor_copy(qv, one[:, 0:6]))
                for c, i in enumerate((1, 3, 0, 2)):
                    ins = dve.tensor_copy(proj1[:, D + c:D + c + 1], qv[:, i:i + 1])
                ins.then_inc(qv_placed, 1)
            masks(0, at([0, 1, 2, 6, 7, 9, 14, 15, 17], own_feed(1) + own_feed(2) + own_feed(3)))
            prepare()
            dve.wait_ge(consts_made, 1)

            def post0(q):
                def divisors():
                    dve.wait_ge(acc_taken, (q + 1) * NB)
                    st.then(dve.tensor_scalar(inv[:, :], Ud, alphac, restc, ALU.mult, ALU.add))
                    st.then(dve.tensor_scalar(zero[:, :], inv[:, :], 0.0, None, ALU.is_equal))
                    st.then(dve.tensor_tensor(inv[:, :], inv[:, :], zero[:, :], ALU.add))
                    st.mark(dve.reciprocal(inv[:, :], inv[:, :]))
                    st.then(dve.tensor_scalar(zero[:, :], zero[:, :], -1.0, 1.0, ALU.mult, ALU.add))
                    st.mark(dve.tensor_tensor(inv[:, :], inv[:, :], zero[:, :], ALU.mult))

                def own_part():
                    st.wait()
                    dve.wait_ge(own_made, q + 1)
                    dve.scalar_tensor_tensor(Uf, Uf, alphac, V3, ALU.mult, ALU.add).then_inc(inv_ready, 1)

                def bias():
                    dve.wait_ge(divided, q + 1)
                    st.then(dve.tensor_tensor(Uf, Uf, bias0_b.unsqueeze(1).broadcast_to([P, S, D]), ALU.add))

                def add():
                    dve.scalar_tensor_tensor(blocks(X, q), Uf, 0.0, blocks(X, q), ALU.max, ALU.add)\
                        .then_inc(post_done, 1)
                    dve.wait_ge(post_done, q + 1)

                def self_loops():
                    dve.wait_ge(mask_made, (q + 1) * T)
                    for s in range(S):
                        ins = dve.tensor_tensor(diagonal(q, s), diagonal(q, s), ident[:, :], ALU.max)
                    st.mark(ins)
                return [divisors, own_part, bias, add, self_loops]

            def stage0(q, more={}):
                post, fed = post0(q - 1), feed(1, q - 1 + Q, q - 1)
                masks(q, at([2, 3, 5, 6, 18, 7, 8, 10, 12, 13, 15], post + fed) | more)
            quarters(dve, 1, Q - 2, stage0, st, STAGE0)
            early = early_of(1)
            stage0(Q - 1, {26: early[0], 28: early[1], 30: lambda: scale_g(1, 0), 31: lambda: scale_g(1, 1)})

            def post1(h, q):
                j = q + h * Q
                n = j + Q

                def divisors():
                    dve.wait_ge(acc_taken, (n + 1) * NB)
                    st.mark(dve.reciprocal(inv[:, :], Ud))

                def residual():
                    if h == 0:
                        dve.wait_ge(input_made, q + 1)
                    else:
                        dve.wait_ge(back, 16 * (q + 1))
                    st.wait()
                    for s in range(S):
                        ins = dve.scalar_tensor_tensor(U3[:, s, 0:D], U3[:, s, 0:D], inv[:, s:s + 1], V[:, s, :], ALU.mult, ALU.add)
                    st.then(ins)

                def scal():
                    if h == 0:
                        dve.wait_ge(f_norm, q + 2 * Q + 1)
                    else:
                        dve.wait_ge(f_norm, q + 3 * Q)
                    scales(n_dev, j + 1, n_scale)

                def elu():
                    dve.wait_ge(exp_made, j + 1)
                    ins = dve.scalar_tensor_tensor(V3, V3, 1.0, mixed3, ALU.min, ALU.add)
                    if h == 0:
                        ins.then_inc(elu_made, 1)
                    else:
                        st.mark(ins)

                def add():
                    if h == 0:
                        dve.wait_ge(half_made, q + 1)
                        ins = dve.tensor_tensor(blocks(X, q), blocks(X, q), V3, ALU.add)
                    else:
                        st.wait()
                        ins = dve.scalar_tensor_tensor(blocks(X, q), V3, 1.0 / HEADS, blocks(X, q), ALU.mult, ALU.add)
                    ins.then_inc(post_done, 1)
                    dve.wait_ge(post_done, n + 1)

                def own_pattern():
                    dve.wait_ge(e_made, (n - Q + 1) * T)
                    for s in range(S):
                        ins = dve.scalar_tensor_tensor(diagonal(q, s), ident[:, :], blocks(dsub, q, 1, s),
                                                       diagonal(q, s), ALU.mult, ALU.add)
                    st.mark(ins)
                steps = [divisors, residual] + statistics(lambda s: U3[:, s, 0:D], n_var) + [scal, elu, add]
                return steps if h == 0 else steps + [own_pattern]

            def late_steps(h):
                first, second = top_of(h)
                return [lambda: (first(), second()), lambda: scale_g(h, Q - 1), lambda: scale_sums(h)]

            other, last = top_of(2), post0(Q - 1)
            run(1, 0, at([1, 2, 4, 6, 7, 9, 10, 13, 14, 16, 21, 23, 24, 25, 28, 31],
                         last[:-1] + feed(1, 2 * Q - 1, Q - 1) + late_steps(1) + other + last[-1:]))
            quarters(dve, 1, Q - 1, lambda q: run(1, q, at([1, 5, 7, 9, 11, 18, 20], post1(0, q - 1))), st, STAGE1)
            run(2, 0, at([1, 3, 5, 8, 10, 17, 20], post1(0, Q - 1)))

            dve.wait_ge(w2_loaded, 16)
            dve.tensor_copy(proj2[:, D:D + 1], qv[:, 5:6])
            dve.tensor_copy(proj2[:, D + 1:D + 2], qv[:, 4:5]).then_inc(qv2_placed, 1)

            def stage2(q, more={}):
                run(2, q, at([1, 4, 6, 8, 10, 16, 18, 13, 19, 21, 23, 28],
                             post1(1, q - 1) + feed(3, q - 1 + 3 * Q, q - 1)) | more)
            quarters(dve, 1, Q - 2, stage2, st, STAGE2)
            stage2(Q - 1, dict(zip((29, 30), early_of(3))))
            scale_g(3, 0)

            def mean_of_all():
                dve.wait_ge(half_summed, Q)
                dve.tensor_scalar(hmean, hmean, 1.0 / N, None, ALU.mult).then_inc(mean_ready, 1)

            def keep_mean():
                dve.wait_ge(mean_spread, 1)
                dve.tensor_copy(mean2, mixed[:, 0:D]).then_inc(mean_kept, 1)
            last = post1(1, Q - 1)

            def ones_and_pattern():
                st.mark(dve.memset(G[:, 0, :, D], 1.0))
                last[-1]()
            run(3, 0, at([1, 2, 3, 5, 7, 12, 13, 15, 16, 18, 21, 22, 23, 24, 25, 27, 29],
                         last[:-1] + feed(3, 4 * Q - 1, Q - 1) + late_steps(3) + [mean_of_all, keep_mean]
                         + [ones_and_pattern]))

            def post2(q):
                def divisors():
                    dve.wait_ge(acc_taken, (q + 3 * Q + 1) * NB)
                    st.then(dve.tensor_scalar(zero[:, :], Ud, 0.0, None, ALU.is_equal))
                    st.then(dve.tensor_tensor(inv[:, :], Ud, zero[:, :], ALU.add))
                    dve.reciprocal(inv[:, :], inv[:, :]).then_inc(inv_ready, 1)

                def sum_():
                    dve.wait_ge(divided, q + Q + 1)
                    st.then(dve.tensor_tensor(Uf, Uf, V3, ALU.add))

                def add():
                    dve.scalar_tensor_tensor(blocks(X, q), Uf, 0.0, blocks(X, q), ALU.max, ALU.add)\
                        .then_inc(post_done, 1)
                    dve.wait_ge(post_done, q + 3 * Q + 1)
                return [divisors, sum_, add]

            def stage3(q):
                run(3, q, at([1, 6, 8, 11, 14, 17], post2(q - 1) + feed(4, q - 1 + 4 * Q, q - 1)))
            quarters(dve, 1, Q - 2, stage3, st, STAGE3)
            stage3(Q - 1)
            for step in post2(Q - 1) + feed(4, 5 * Q - 1, Q - 1):
                step()

            def post3(q):
                dve.wait_ge(acc_taken, (q + 4 * Q + 1) * NB)
                st.then(dve.tensor_scalar(zero[:, :], Ud, 0.0, None, ALU.is_equal))
                st.then(dve.tensor_tensor(inv[:, :], Ud, zero[:, :], ALU.add))
                st.then(dve.reciprocal(inv[:, :], inv[:, :]))
                st.then(dve.tensor_scalar(zero[:, :], zero[:, :], -1.0, 1.0, ALU.mult, ALU.add))
                st.then(dve.tensor_tensor(inv[:, :], inv[:, :], zero[:, :], ALU.mult))
                if not fixed(q):
                    dve.wait_ge(stored, q * 16)
                for s in range(S):
                    ins = dve.scalar_tensor_tensor(V[:, s, :], U3[:, s, 0:D], inv[:, s:s + 1], blocks(X, q, 1, s)[:, 0, :],
                                                   ALU.mult, ALU.add)
                ins.then_inc(post_done, 1)
            post3(0)
            quarters(dve, 1, Q - 2, post3, st, 5)
            dve.wait_ge(stored, (Q - 1) * 16)
            for b in range(NB):
                dve.wait_ge(acc_taken, (5 * Q - 1) * NB + b + 1)
                some = slice(3 * b, 3 * b + width(b))
                z, i = zero[:, some], inv[:, some]
                st.then(dve.tensor_scalar(z, U3[:, some, D], 0.0, None, ALU.is_equal))
                st.then(dve.tensor_tensor(i, U3[:, some, D], z, ALU.add))
                st.then(dve.reciprocal(i, i))
                st.then(dve.tensor_scalar(z, z, -1.0, 1.0, ALU.mult, ALU.add))
                st.then(dve.tensor_tensor(i, i, z, ALU.mult))
                for s in range(3 * b, 3 * b + width(b)):
                    ins = dve.scalar_tensor_tensor(V[:, s, :], U3[:, s, 0:D], inv[:, s:s + 1], X[:, (Q - 1) * S + s, :],
                                                   ALU.mult, ALU.add)
                ins.then_inc(last_made, 1)


def kernel(**inputs):
    import numpy as np
    import concourse.bacc as bacc
    from concourse.bass_utils import run_bass_kernel_spmd

    nc = bacc.Bacc("TRN2", target_bir_lowering=False, num_devices=1)
    g = {k: np.asarray(v) for k, v in inputs.items()}
    given = {
        "x": g["x"], "adj": g["adj"], "adj_t": g["adj"].T, "diag": g["adj"].diagonal().reshape(-1, P).T,
        "alpha": g["L0_gnn_alpha"],
        "w0_t": g["L0_gnn_W"].T, "bias0": g["L0_gnn_b"],
        "ff0": g["L1_gnn_ff0_w"], "ff0_t": g["L1_gnn_ff0_w"].transpose(0, 2, 1),
        "ff1_t": g["L1_gnn_ff1_w"].transpose(0, 2, 1), "attn": g["L1_gnn_attn_w"].reshape(4, P).T,
        "g1": g["L1_gnn_g1"], "b1": g["L1_gnn_b1"], "g2": g["L1_gnn_g2"], "b2": g["L1_gnn_b2"],
        "w2": g["L2_gnn_W"], "w2_t": g["L2_gnn_W"].T, "a2": g["L2_gnn_a"].reshape(2, P).T,
    }
    arrays, args = {}, []
    for name, a in given.items():
        a = np.ascontiguousarray(a)
        arrays[f"in_{name}"] = a
        args.append(nc.dram_tensor(f"in_{name}", a.shape, mybir.dt.from_np(a.dtype), kind="ExternalInput").ap())
    args.append(nc.dram_tensor("out_x", g["x"].shape, F32, kind="ExternalOutput").ap())
    args.append(nc.dram_tensor("inputs1", (P, g["x"].size // P), F32, kind="Internal").ap())
    graph_layers(nc, *args)
    r = run_bass_kernel_spmd(nc, [arrays], core_ids=[0])
    return r.results[0]["out_x"]
```
